# Optimizing a Trainium2 kernel written in Bass

```python
import numpy as np
import jax
import jax.numpy as jnp

def _softmax(x, axis=-1):
    return jax.nn.softmax(x, axis=axis)

def _gelu(x):
    return jax.nn.gelu(x, approximate=True)

def _silu(x):
    return jax.nn.silu(x)

def _sigmoid(x):
    return jax.nn.sigmoid(x)

def _layernorm(x, axis=-1, eps=1e-05):
    m = jnp.mean(x, axis=axis, keepdims=True)
    v = jnp.var(x, axis=axis, keepdims=True)
    return (x - m) / jnp.sqrt(v + eps)

def _scatter_add(tgt, idx, src, axis=0):
    return tgt.at[idx].add(src)

def _segment_sum(src, seg, n):
    return jax.ops.segment_sum(src, seg, n)
kernel_name = 'mk_cond_resid_d4_seqx_r2_5446cb'

def setup_inputs(seed: int=0):
    np.random.seed(seed)
    _w = jnp.asarray

    def _rec_inputs():
        import jax
        import jax.numpy as jnp
        _rk = jax.random.key(seed)
        x = -0.000125 + 0.9999 * jax.random.normal(jax.random.fold_in(_rk, 1), (32, 128, 2048), jnp.float32)
        _lenS = 128 - jax.random.randint(jax.random.fold_in(_rk, 7), (32,), 0, max(1, 128 // 4) + 1, jnp.int32)
        _lenS2 = 128 - jax.random.randint(jax.random.fold_in(_rk, 8), (32,), 0, max(1, 128 // 4) + 1, jnp.int32)
        cond_128 = 0.0061147 + 1.02565 * jax.random.normal(jax.random.fold_in(_rk, 11), (32, 128), jnp.float32)
        fside_S_0 = -0.022604 + 0.987366 * jax.random.normal(jax.random.fold_in(_rk, 12), (128,), jnp.float32)
        return (x, cond_128, fside_S_0)
    x, cond_128, fside_S_0 = _rec_inputs()

    def _L0_cond_setup():
        import jax, jax.numpy as jnp
        import numpy as np
        from jax import lax
        N, C_IN, L = (32, 128, 2048)
        C_OUT, K, GROUPS = (128, 9, 4)
        C_DIM, PAD, STRIDE = (128, 4, 1)
        key = jax.random.key(seed)
        k1, k2, k3, k4, k5 = jax.random.split(key, 5)
        x = jax.random.normal(k1, (N, C_IN, L), dtype=jnp.float32)
        c = jax.random.normal(k2, (N, C_DIM), dtype=jnp.float32)
        weight = jax.random.normal(k3, (C_OUT, C_IN // GROUPS, K), dtype=jnp.float32)
        c_weight = jax.random.normal(k4, (C_OUT, C_DIM), dtype=jnp.float32)
        bias = jax.random.normal(k5, (C_OUT,), dtype=jnp.float32)
        return {'x': x, 'c': c, 'weight': weight, 'c_weight': c_weight, 'bias': bias}
    _L0_cond_all = _L0_cond_setup()
    _L0_cond_in = {k: v for k, v in _L0_cond_all.items() if k in ('weight', 'c_weight')}
    del _L0_cond_all

    def _L1_cond_setup():
        import jax, jax.numpy as jnp
        import numpy as np
        K = 8
        T = 1.0
        D_EMBD = 128
        IN_C = 128
        OUT_C = 128
        BS = 32
        H = 2048
        HID = 128
        key = jax.random.key(seed)
        ks = jax.random.split(key, 10)
        s = lambda fan_in: 1.0 / np.sqrt(fan_in)
        return {'x': jax.random.normal(ks[0], (BS, IN_C, H), dtype=jnp.float32), 'embedding': jax.random.normal(ks[1], (BS, D_EMBD), dtype=jnp.float32), 'W0': jax.random.normal(ks[2], (D_EMBD, HID), dtype=jnp.float32) * s(D_EMBD), 'b0': jnp.zeros((HID,), dtype=jnp.float32), 'W1': jax.random.normal(ks[3], (HID, HID), dtype=jnp.float32) * s(HID), 'b1': jnp.zeros((HID,), dtype=jnp.float32), 'W2': jax.random.normal(ks[4], (HID, K), dtype=jnp.float32) * s(HID), 'b2': jnp.zeros((K,), dtype=jnp.float32), 'weight': jax.random.normal(ks[5], (K, OUT_C, IN_C, 1), dtype=jnp.float32) * s(IN_C), 'bias_k': jax.random.normal(ks[6], (K, OUT_C), dtype=jnp.float32) * 0.1}
    _L1_cond_all = _L1_cond_setup()
    _L1_cond_in = {k: v for k, v in _L1_cond_all.items() if k in ('W0', 'b0', 'W1', 'b1', 'W2', 'b2', 'weight', 'bias_k')}
    del _L1_cond_all

    def _L2_cond_setup():
        import jax, jax.numpy as jnp
        import numpy as np
        K = 8
        T = 1.0
        D_EMBD = 128
        IN_C = 128
        OUT_C = 128
        BS = 32
        H = 2048
        HID = 128
        key = jax.random.key(seed)
        ks = jax.random.split(key, 10)
        s = lambda fan_in: 1.0 / np.sqrt(fan_in)
        return {'x': jax.random.normal(ks[0], (BS, IN_C, H), dtype=jnp.float32), 'embedding': jax.random.normal(ks[1], (BS, D_EMBD), dtype=jnp.float32), 'W0': jax.random.normal(ks[2], (D_EMBD, HID), dtype=jnp.float32) * s(D_EMBD), 'b0': jnp.zeros((HID,), dtype=jnp.float32), 'W1': jax.random.normal(ks[3], (HID, HID), dtype=jnp.float32) * s(HID), 'b1': jnp.zeros((HID,), dtype=jnp.float32), 'W2': jax.random.normal(ks[4], (HID, K), dtype=jnp.float32) * s(HID), 'b2': jnp.zeros((K,), dtype=jnp.float32), 'weight': jax.random.normal(ks[5], (K, OUT_C, IN_C, 1), dtype=jnp.float32) * s(IN_C), 'bias_k': jax.random.normal(ks[6], (K, OUT_C), dtype=jnp.float32) * 0.1}
    _L2_cond_all = _L2_cond_setup()
    _L2_cond_in = {k: v for k, v in _L2_cond_all.items() if k in ('W0', 'b0', 'W1', 'b1', 'W2', 'b2', 'weight', 'bias_k')}
    del _L2_cond_all

    def _L3_cond_setup():
        import jax, jax.numpy as jnp
        import numpy as np
        from jax import lax
        N, C_IN, L = (32, 128, 2048)
        C_OUT, K, GROUPS = (128, 9, 4)
        C_DIM, PAD, STRIDE = (128, 4, 1)
        key = jax.random.key(seed)
        k1, k2, k3, k4, k5 = jax.random.split(key, 5)
        x = jax.random.normal(k1, (N, C_IN, L), dtype=jnp.float32)
        c = jax.random.normal(k2, (N, C_DIM), dtype=jnp.float32)
        weight = jax.random.normal(k3, (C_OUT, C_IN // GROUPS, K), dtype=jnp.float32)
        c_weight = jax.random.normal(k4, (C_OUT, C_DIM), dtype=jnp.float32)
        bias = jax.random.normal(k5, (C_OUT,), dtype=jnp.float32)
        return {'x': x, 'c': c, 'weight': weight, 'c_weight': c_weight, 'bias': bias}
    _L3_cond_all = _L3_cond_setup()
    _L3_cond_in = {k: v for k, v in _L3_cond_all.items() if k in ('weight', 'c_weight')}
    del _L3_cond_all
    return {'x': x, 'cond_128': cond_128, 'fside_S_0': fside_S_0, 'L0_cond_weight': _L0_cond_in['weight'], 'L0_cond_c_weight': _L0_cond_in['c_weight'], 'L1_cond_W0': _L1_cond_in['W0'], 'L1_cond_b0': _L1_cond_in['b0'], 'L1_cond_W1': _L1_cond_in['W1'], 'L1_cond_b1': _L1_cond_in['b1'], 'L1_cond_W2': _L1_cond_in['W2'], 'L1_cond_b2': _L1_cond_in['b2'], 'L1_cond_weight': _L1_cond_in['weight'], 'L1_cond_bias_k': _L1_cond_in['bias_k'], 'L2_cond_W0': _L2_cond_in['W0'], 'L2_cond_b0': _L2_cond_in['b0'], 'L2_cond_W1': _L2_cond_in['W1'], 'L2_cond_b1': _L2_cond_in['b1'], 'L2_cond_W2': _L2_cond_in['W2'], 'L2_cond_b2': _L2_cond_in['b2'], 'L2_cond_weight': _L2_cond_in['weight'], 'L2_cond_bias_k': _L2_cond_in['bias_k'], 'L3_cond_weight': _L3_cond_in['weight'], 'L3_cond_c_weight': _L3_cond_in['c_weight']}

def reference(x, cond_128, fside_S_0, L0_cond_weight, L0_cond_c_weight, L1_cond_W0, L1_cond_b0, L1_cond_W1, L1_cond_b1, L1_cond_W2, L1_cond_b2, L1_cond_weight, L1_cond_bias_k, L2_cond_W0, L2_cond_b0, L2_cond_W1, L2_cond_b1, L2_cond_W2, L2_cond_b2, L2_cond_weight, L2_cond_bias_k, L3_cond_weight, L3_cond_c_weight):
    import jax
    import jax.numpy as jnp

    def _L0_cond_ref(x, c, weight, c_weight, bias):
        import jax, jax.numpy as jnp
        import numpy as np
        from jax import lax
        N, C_IN, L = (32, 128, 2048)
        C_OUT, K, GROUPS = (128, 9, 4)
        C_DIM, PAD, STRIDE = (128, 4, 1)
        out = lax.conv_general_dilated(x, weight, window_strides=(STRIDE,), padding=[(PAD, PAD)], dimension_numbers=('NCH', 'OIH', 'NCH'), feature_group_count=GROUPS)
        ctx = jnp.einsum('nd,od->no', c, c_weight)
        out = out + ctx[:, :, None] + bias[None, :, None]
        return out

    def _L1_cond_ref(x, embedding, W0, b0, W1, b1, W2, b2, weight, bias_k):
        import jax, jax.numpy as jnp
        import numpy as np
        K = 8
        T = 1.0
        D_EMBD = 128
        IN_C = 128
        OUT_C = 128
        BS = 32
        H = 2048
        HID = 128
        h = jax.nn.gelu(embedding @ W0 + b0, approximate=False)
        h = jax.nn.gelu(h @ W1 + b1, approximate=False)
        att = jax.nn.softmax((h @ W2 + b2) / T, axis=-1)
        agg_w = jnp.einsum('bk,koi->boi', att, weight[..., 0])
        agg_b = att @ bias_k
        out = jnp.einsum('boi,bih->boh', agg_w, x) + agg_b[:, :, None]
        return out

    def _L2_cond_ref(x, embedding, W0, b0, W1, b1, W2, b2, weight, bias_k):
        import jax, jax.numpy as jnp
        import numpy as np
        K = 8
        T = 1.0
        D_EMBD = 128
        IN_C = 128
        OUT_C = 128
        BS = 32
        H = 2048
        HID = 128
        h = jax.nn.gelu(embedding @ W0 + b0, approximate=False)
        h = jax.nn.gelu(h @ W1 + b1, approximate=False)
        att = jax.nn.softmax((h @ W2 + b2) / T, axis=-1)
        agg_w = jnp.einsum('bk,koi->boi', att, weight[..., 0])
        agg_b = att @ bias_k
        out = jnp.einsum('boi,bih->boh', agg_w, x) + agg_b[:, :, None]
        return out

    def _L3_cond_ref(x, c, weight, c_weight, bias):
        import jax, jax.numpy as jnp
        import numpy as np
        from jax import lax
        N, C_IN, L = (32, 128, 2048)
        C_OUT, K, GROUPS = (128, 9, 4)
        C_DIM, PAD, STRIDE = (128, 4, 1)
        out = lax.conv_general_dilated(x, weight, window_strides=(STRIDE,), padding=[(PAD, PAD)], dimension_numbers=('NCH', 'OIH', 'NCH'), feature_group_count=GROUPS)
        ctx = jnp.einsum('nd,od->no', c, c_weight)
        out = out + ctx[:, :, None] + bias[None, :, None]
        return out
    x = x + _L0_cond_ref(x, cond_128, L0_cond_weight, L0_cond_c_weight, fside_S_0)
    x = x + _L1_cond_ref(x, cond_128, L1_cond_W0, L1_cond_b0, L1_cond_W1, L1_cond_b1, L1_cond_W2, L1_cond_b2, L1_cond_weight, L1_cond_bias_k)
    x = x + _L2_cond_ref(x, cond_128, L2_cond_W0, L2_cond_b0, L2_cond_W1, L2_cond_b1, L2_cond_W2, L2_cond_b2, L2_cond_weight, L2_cond_bias_k)
    x = x + _L3_cond_ref(x, cond_128, L3_cond_weight, L3_cond_c_weight, fside_S_0)
    return x

_drawn_inputs = setup_inputs


def setup_inputs(seed=0):
    import zlib

    import numpy as np

    out = dict(_drawn_inputs(seed))
    spreads = {'L1_cond_b0': (0.0, 0.699),
     'L1_cond_b1': (0.0, 0.491),
     'L1_cond_b2': (0.0, 0.386),
     'L2_cond_b0': (0.0, 0.746),
     'L2_cond_b1': (0.0, 0.38),
     'L2_cond_b2': (0.0, 0.436)}
    factors = {'L1_cond_bias_k': 38.07, 'L2_cond_bias_k': 40.526}
    for name, (base, spread) in spreads.items():
        noise = np.random.default_rng([zlib.crc32(name.encode()), seed]).standard_normal(out[name].shape)
        drawn = base * np.exp(spread * noise) if base else spread * noise
        out[name] = jnp.asarray(drawn.astype(out[name].dtype))
    for name, factor in factors.items():
        out[name] = (out[name] * factor).astype(out[name].dtype)
    return out
```

```python
from contextlib import ExitStack

import concourse.bass as bass
from concourse import mybir

F32 = mybir.dt.float32
F32R = mybir.dt.float32r
ALU = mybir.AluOpType
ACT = mybir.ActivationFunctionType
AX = mybir.AxisListType

N, C, L = 32, 128, 2048
G = 4
GC = C // G
TAPS, PAD = 9, 4
PH = C // GC
S = L // PH
JB = 3
SLOTS = PH * JB + PH - 1
FIRST = PH - 1
K = 8
D = 128
DMA = 16
RELAY = G * DMA
TAB = 2 * K + 2


def conditioned_residual_kernel(nc, x, cond, side, conv0_w, ctx0_w, mix1, mix2, conv3_w, ctx3_w, out):
    ctx = ExitStack()
    with ctx:
        def sb(name, shape, dt=F32):
            return ctx.enter_context(nc.sbuf_tensor(name, shape, dt))

        def sem(name):
            return ctx.enter_context(nc.semaphore(name))

        x_in = [sb(f"x_in{i}", [C, L]) for i in range(2)]
        x_phase = sb("x_phase", [C, PH, S])
        x_tap = sb("x_tap", [C, G, S])
        x_hi = [sb(f"x_hi{i}", [C, G, S + 2], F32R) for i in range(2)]
        x_lo = [sb(f"x_lo{i}", [C, G, S + 2], F32R) for i in range(2)]
        y_tap = sb("y_tap", [C, G, S])
        y_phase = sb("y_phase", [C, PH, S])
        y_hi = sb("y_hi", [C, PH, S], F32R)
        y_lo = sb("y_lo", [C, PH, S], F32R)
        z_phase = sb("z_phase", [C, PH, S])
        z_tap = sb("z_tap", [C, G, S])
        z_hi = [sb(f"z_hi{i}", [C, G, S + 2], F32R) for i in range(2)]
        z_lo = [sb(f"z_lo{i}", [C, G, S + 2], F32R) for i in range(2)]
        out_sb = [sb(f"out_sb{i}", [C, L]) for i in range(2)]

        taps0_hi = sb("taps0_hi", [C, JB, G, C], F32R)
        taps0_lo = sb("taps0_lo", [C, JB, G, C], F32R)
        taps3_hi = sb("taps3_hi", [C, JB, G, C], F32R)
        taps3_lo = sb("taps3_lo", [C, JB, G, C], F32R)
        mix1_w = sb("mix1_w", [C, K, C])
        mix2_wT = sb("mix2_wT", [C, K, C])
        mat1 = sb("mat1", [C, C])
        mat2T = sb("mat2T", [C, C])
        acc1 = sb("acc1", [C, C])
        acc2 = sb("acc2", [C, C])
        prod_hi = sb("prod_hi", [C, C], F32R)
        prod_lo = sb("prod_lo", [C, C], F32R)
        mix_tab = sb("mix_tab", [C, N, TAB])
        mix_cur = [sb(f"mix_cur{i}", [C, TAB]) for i in range(2)]
        mix_bias = [sb(f"mix_bias{i}", [C, 1]) for i in range(2)]
        bias_tab = sb("bias_tab", [C, N + 2, 2 * G])
        bias_cur = [sb(f"bias_cur{i}", [C, 2 * G]) for i in range(2)]
        ident = sb("ident", [C, C])
        ones = sb("ones", [GC, C])

        z0 = z_tap[:, :, :].rearrange("c g s -> c (g s)")
        padded3 = z0[:, 0:GC * SLOTS].rearrange("o (c k) -> o c k", k=SLOTS)
        conv3_in = z0[:, 512:512 + GC * TAPS].rearrange("o (c k) -> o c k", k=TAPS)
        padded0 = z0[:, 1024:1024 + GC * SLOTS].rearrange("o (c k) -> o c k", k=SLOTS)
        conv0_in = z0[:, 1536:1536 + GC * TAPS].rearrange("o (c k) -> o c k", k=TAPS)
        windows = z_phase[:, :, :].rearrange("c p s -> c (p s)")[:, 0:JB * PH * C]\
            .rearrange("o (j q m) -> o j q m", j=JB, q=PH)
        o0 = out_sb[0]
        ctx_in = [o0[:, 128 * l:128 * l + 128] for l in range(2)]
        ctx_rep = [o0[:, 256 + 512 * l:256 + 512 * l + 512] for l in range(2)]
        cond_in = o0[0:N, 1280:1408]
        condT = o0[:, 1408:1440]
        side_in = o0[0:1, 1440:1568]
        o1 = out_sb[1]
        side_rep = [o1[0:1, 512 * l:512 * l + 512] for l in range(2)]
        mlp_w = [[o1[:, 1024 + 256 * l + 128 * m:1152 + 256 * l + 128 * m] for m in range(2)] for l in range(2)]
        mlp_b = [[o1[:, 1536 + 2 * l + m:1537 + 2 * l + m] for m in range(2)] for l in range(2)]
        key_w = [o1[:, 1544 + K * l:1544 + K * l + K] for l in range(2)]
        key_b = [o1[0:1, 1560 + K * l:1560 + K * l + K] for l in range(2)]
        bias_k = [o1[0:K, 1576 + 128 * l:1704 + 128 * l] for l in range(2)]
        hid = [[o1[:, 1832 + 64 * l + 32 * m:1864 + 64 * l + 32 * m] for m in range(2)] for l in range(2)]
        soft = sb("soft", [N, 64])
        att_exp = [soft[:, K * l:K * l + K] for l in range(2)]
        att = [soft[:, 16 + K * l:16 + K * l + K] for l in range(2)]
        att_max = [soft[:, 32 + l:33 + l] for l in range(2)]
        att_sum = [soft[:, 34 + l:35 + l] for l in range(2)]
        att_inv = [soft[:, 36 + l:37 + l] for l in range(2)]
        attT = [soft[0:K, 0:1]] * 2
        attT_sb = sb("attT_sb", [K, 2, N])
        spread = sb("spread", [N, N, 2 * K])
        mix2_in = y_phase[:, :, :].rearrange("c p s -> c (p s)")[:, 0:K * C].rearrange("o (k i) -> o k i", i=C)

        ps = ctx.enter_context(nc.psum_tensor("ps", [C, 8, 512], F32))

        conv_w_in = [sem(f"conv_w_in{l}") for l in range(2)]
        ctx_w_in = [sem(f"ctx_w_in{l}") for l in range(2)]
        cond_arrived = sem("cond_arrived")
        side_arrived = sem("side_arrived")
        mlp_arrived = sem("mlp_arrived")
        mix1_arrived = sem("mix1_arrived")
        mix2_arrived = sem("mix2_arrived")
        ident_step = sem("ident_step")
        padded_step = [sem(f"padded_step{l}") for l in range(2)]
        windows_cut = [sem(f"windows_cut{l}") for l in range(2)]
        windows_done = [sem(f"windows_done{l}") for l in range(2)]
        taps_hi_done = [sem(f"taps_hi_done{l}") for l in range(2)]
        taps_lo_done = [sem(f"taps_lo_done{l}") for l in range(2)]
        condT_psum = sem("condT_psum")
        condT_done = sem("condT_done")
        ctxT_psum = [sem(f"ctxT_psum{l}") for l in range(2)]
        ctx_rep_done = [sem(f"ctx_rep_done{l}") for l in range(2)]
        bias_psum = [sem(f"bias_psum{l}") for l in range(2)]
        bias_tab_done = [sem(f"bias_tab_done{l}") for l in range(2)]
        hidden_psum = sem("hidden_psum")
        hidden_done = sem("hidden_done")
        logits_psum = sem("logits_psum")
        max_done = sem("max_done")
        exp_done = sem("exp_done")
        att_step = sem("att_step")
        spread_done = sem("spread_done")
        attT_psum = sem("attT_psum")
        attT_done = sem("attT_done")
        tab_psum = sem("tab_psum")
        agg_psum = sem("agg_psum")
        mix_tab_done = sem("mix_tab_done")
        mix2T_psum = sem("mix2T_psum")
        mix2T_done = sem("mix2T_done")
        halo_done = sem("halo_done")

        x_loaded = [sem(f"x_loaded{i}") for i in range(2)]
        x_phased = sem("x_phased")
        x_relaid = sem("x_relaid")
        x_split = sem("x_split")
        conv0_done = sem("conv0_done")
        y_evac = sem("y_evac")
        y_relaid = sem("y_relaid")
        y_split = sem("y_split")
        mats_step = sem("mats_step")
        cur_done = sem("cur_done")
        prod_done = sem("prod_done")
        prod_split = sem("prod_split")
        mix_done = sem("mix_done")
        z_evac = sem("z_evac")
        z_relaid = sem("z_relaid")
        z_split = sem("z_split")
        conv3_done = sem("conv3_done")
        bias_done = sem("bias_done")
        out_evac = sem("out_evac")
        out_stored = [sem(f"out_stored{i}") for i in range(2)]

        block = ctx.enter_context(nc.Block())

        def wait(eng, s, value):
            if not isinstance(value, int) or value > 0:
                eng.wait_ge(s, value)

        class Step:

            def __init__(self, half, parity):
                self.half, self.parity, self.i = half, parity, 2 * half + parity

            def has(self, d):
                return not isinstance(self.half, int) or 0 <= self.i + d < N

            def par(self, d):
                return (self.parity + d) % 2

            def pair(self, d):
                return self.half + (self.parity + d) // 2

        LOOP = (2, (N - 2) // 2)

        def steps(eng, one):
            for i in range(2 * LOOP[0]):
                one(Step(i // 2, i % 2) if i else first)
            with eng.Fori(LOOP[0], LOOP[1]) as half:
                one(Step(half, 0))
                one(Step(half, 1))
            for i in range(2 * LOOP[1], N + 2):
                one(Step(i // 2, i % 2))

        first = Step(0, 0)

        @block.sync
        def _(sp):
            def count(value):
                return value if isinstance(value, int) else sp.snap(value)

            def load_x(t, d):
                b = count(t.i + d)
                read = count(t.i + d - 1)
                src = x[b]
                wait(sp, x_phased, read)
                sp.dma_start(x_in[t.par(d)][:, :], src).then_inc(x_loaded[t.par(d)], DMA)

            def relay_x(t, d):
                written, read = count(t.i + d + 1), count(2 * (t.i + d))
                wait(sp, x_split, read)
                wait(sp, x_phased, written)
                for g in range(G):
                    sp.dma_start(x_tap[:, g, :], x_phase[GC * g:GC * g + GC, :, :]).then_inc(x_relaid, DMA)

            def relay_y(t):
                read, written = count(2 * t.i), [count(G * t.i + g + 1) for g in range(G)]
                wait(sp, y_split, read)
                for g in range(G):
                    wait(sp, y_evac, written[g])
                    sp.dma_start(y_phase[GC * g:GC * g + GC, :, :], y_tap[:, g, :]).then_inc(y_relaid, DMA)

            def relay_z(t):
                written, read = count(2 * t.i), count(2 * (t.i - 1))
                wait(sp, z_evac, written)
                wait(sp, z_split, read)
                for g in range(G):
                    sp.dma_start(z_tap[:, g, :], z_phase[GC * g:GC * g + GC, :, :]).then_inc(z_relaid, DMA)

            def store(t):
                b = count(t.i - 2)
                written = count(G * PH * (t.i - 1))
                dst = out[b]
                wait(sp, out_evac, written)
                sp.dma_start(dst, out_sb[t.par(0)][:, :]).then_inc(out_stored[t.par(0)], DMA)

            def one(t):
                if t.has(2):
                    load_x(t, 2)
                if t.has(1):
                    relay_x(t, 1)
                if t.has(0):
                    relay_y(t)
                if t.has(-1):
                    relay_z(t)
                if t.has(-2):
                    store(t)

            sp.dma_start(x_in[0][:, :], x[0]).then_inc(x_loaded[0], DMA)
            sp.dma_start(mlp_w[0][0], mix1[0]).then_inc(mlp_arrived, DMA)
            sp.dma_start(mlp_w[1][0], mix2[0]).then_inc(mlp_arrived, DMA)
            sp.dma_start(mlp_w[0][1], mix1[2]).then_inc(mlp_arrived, DMA)
            sp.dma_start(mlp_w[1][1], mix2[2]).then_inc(mlp_arrived, DMA)
            relay_x(first, 0)
            load_x(first, 1)
            sp.dma_start(mix1_w[:, :, :], mix1[6].rearrange("k o i -> o k i")).then_inc(mix1_arrived, DMA)
            sp.dma_start(mix2_in, mix2[6].rearrange("k o i -> o k i")).then_inc(mix2_arrived, DMA)
            sp.wait_ge(mix2T_psum, 2)
            steps(sp, one)
            sp.wait_ge(out_stored[0], DMA * (N // 2))
            sp.wait_ge(out_stored[1], DMA * (N // 2))

        @block.gpsimd
        def _(pool):
            pool.memset(ident[:, :], 0.0).then_inc(ident_step, 1)
            pool.wait_ge(ident_step, 1)
            pool.affine_select(out=ident[:, :], in_=ident[:, :], compare_op=ALU.not_equal, fill=1.0, base=0,
                               pattern=[[-1, C]], channel_multiplier=1).then_inc(ident_step, 1)
            pool.memset(ones[:, :], 1.0).then_inc(ident_step, 1)
            pool.memset(bias_tab[:, :, :], 0.0).then_inc(ident_step, 1)
            for buf in x_hi + x_lo + z_hi + z_lo:
                pool.memset(buf[:, :, 0:S + 2:S + 1].bitcast(F32), 0.0).then_inc(halo_done, 1)

        HALOS = 8

        @block.scalar
        def _(act):
            def phase_x(t, d):
                b = t.i + d
                act.wait_ge(x_loaded[t.par(d)], DMA * (t.pair(d) + 1))
                wait(act, x_relaid, RELAY * b)
                act.activation(x_phase[:, :, :], x_in[t.par(d)][:, :].rearrange("c (s p) -> c p s", p=PH),
                               ACT.Copy).then_inc(x_phased, 1)

            def copy_bias(t):
                wait(act, y_evac, G * (t.i - 1))
                wait(act, out_evac, G * PH * (t.i - 3))
                act.activation(bias_cur[t.par(0)][:, :], bias_tab[:, t.i, :], ACT.Copy).then_inc(bias_done, 1)

            def evac_y(t, g):
                b = t.i
                act.wait_ge(conv0_done, G * b + g + 1)
                act.activation(y_tap[:, g, :], ps[:, g, :], ACT.Identity,
                               bias=bias_cur[t.par(0)][:, g:g + 1]).then_inc(y_evac, 1)

            def evac_ys(t):
                b = t.i
                act.wait_ge(bias_done, b + 1)
                wait(act, y_relaid, RELAY * b)
                for g in range(G):
                    evac_y(t, g)

            def evac_z(t):
                b = t.i - 1
                wait(act, z_relaid, RELAY * b)
                act.wait_ge(prod_split, 3 * b + 3)
                for h in range(2):
                    act.wait_ge(mix_done, PH * b + 2 * h + 2)
                    bank = 4 if h == 0 else 0
                    act.activation(z_phase[:, 2 * h:2 * h + 2, :], ps[:, bank:bank + 2, :], ACT.Identity,
                                   bias=mix_bias[t.par(-1)][:, :]).then_inc(z_evac, 1)

            def evac_out(t):
                b = t.i - 2
                act.wait_ge(bias_done, t.i + 1)
                wait(act, out_stored[t.par(0)], DMA * t.pair(-2))
                o = out_sb[t.par(0)][:, :].rearrange("c (s p) -> c p s", p=PH)
                for g in range(G):
                    act.wait_ge(conv3_done, G * b + g + 1)
                    for q in range(PH):
                        act.activation(o[GC * g:GC * g + GC, q, :], ps[GC * q:GC * q + GC, 2 + g, :], ACT.Identity,
                                       bias=bias_cur[t.par(0)][GC * q:GC * q + GC, G + g:G + g + 1])\
                           .then_inc(out_evac, 1)

            def one(t):
                if t is not first:
                    copy_bias(t)
                if t.has(1):
                    phase_x(t, 1)
                if t.has(0) and t is not first:
                    evac_ys(t)
                if t.has(-1):
                    evac_z(t)
                if t.has(-2):
                    evac_out(t)

            act.dma_start(conv0_in, conv0_w).then_inc(conv_w_in[0], DMA)
            act.dma_start(cond_in, cond).then_inc(cond_arrived, DMA)
            act.dma_start(ctx_in[0], ctx0_w).then_inc(ctx_w_in[0], DMA)
            act.dma_start(side_in, side.rearrange("(a c) -> a c", a=1)).then_inc(side_arrived, DMA)
            for l, m in enumerate((mix1, mix2)):
                act.dma_start(mlp_b[l][0], m[1].rearrange("(c a) -> c a", a=1)).then_inc(mlp_arrived, DMA)
                act.dma_start(mlp_b[l][1], m[3].rearrange("(c a) -> c a", a=1)).then_inc(mlp_arrived, DMA)
                act.dma_start(key_w[l], m[4]).then_inc(mlp_arrived, DMA)
                act.dma_start(key_b[l], m[5].rearrange("(a k) -> a k", a=1)).then_inc(mlp_arrived, DMA)
                act.dma_start(bias_k[l], m[7]).then_inc(mlp_arrived, DMA)
            act.dma_start(conv3_in, conv3_w).then_inc(conv_w_in[1], DMA)
            act.dma_start(ctx_in[1], ctx3_w).then_inc(ctx_w_in[1], DMA)
            phase_x(first, 0)
            for j in range(JB):
                act.wait_ge(windows_done[0], j + 1)
                act.activation(taps0_hi[:, j, :, :].rearrange("r g (o q) -> r g q o", q=PH),
                               ps[:, j, :].rearrange("r (q g o) -> r g q o", q=PH, g=G), ACT.Copy)\
                   .then_inc(taps_hi_done[0], 1)
            act.wait_ge(bias_tab_done[0], 1)
            copy_bias(first)
            act.wait_ge(bias_done, 1)
            for m in range(2):
                act.wait_ge(hidden_psum, m + 1)
                for l in range(2):
                    act.activation(hid[l][m], ps[:, 6, 64 + 32 * (2 * m + l):96 + 32 * (2 * m + l)], ACT.Gelu,
                                   bias=mlp_b[l][m]).then_inc(hidden_done, 1)
                evac_y(first, m)
            act.wait_ge(max_done, 2)
            for l in range(2):
                act.activation(att_exp[l], ps[0:N, 6, 192 + K * l:192 + K * l + K], ACT.Exp,
                               bias=att_max[l], accum_out=att_sum[l]).then_inc(exp_done, 1)
            evac_y(first, 2)
            evac_y(first, 3)
            for j in range(JB):
                act.wait_ge(windows_done[1], j + 1)
                act.activation(taps3_hi[:, j, :, :].rearrange("r g (q o) -> r g q o", q=PH),
                               ps[:, j, :].rearrange("r (q g o) -> r g q o", q=PH, g=G), ACT.Copy)\
                   .then_inc(taps_hi_done[1], 1)
            for h in range(2):
                act.wait_ge(mix2T_psum, h + 1)
                act.activation(mix2_wT[:, 4 * h:4 * h + 4, :].rearrange("i k o -> i (k o)"), ps[:, 4 + h, :],
                               ACT.Copy).then_inc(mix2T_done, 1)
            act.wait_ge(bias_tab_done[1], 1)
            steps(act, one)

        @block.vector
        def _(dve):
            def split_x(t, d):
                b, p = t.i + d, t.par(d)
                dve.wait_ge(x_relaid, RELAY * (b + 1))
                wait(dve, conv0_done, G * (b - 1))
                dve.tensor_copy(x_hi[p][:, :, 1:S + 1], x_tap[:, :, :]).then_inc(x_split, 1)
                dve.wait_ge(x_split, 2 * b + 1)
                dve.tensor_tensor(out=x_lo[p][:, :, 1:S + 1], in0=x_tap[:, :, :],
                                  in1=x_hi[p][:, :, 1:S + 1].bitcast(F32), op=ALU.subtract).then_inc(x_split, 1)

            def split_y(t):
                b = t.i
                dve.wait_ge(y_relaid, RELAY * (b + 1))
                wait(dve, mix_done, PH * b)
                dve.tensor_copy(y_hi[:, :, :], y_phase[:, :, :]).then_inc(y_split, 1)
                dve.wait_ge(y_split, 2 * b + 1)
                dve.tensor_tensor(out=y_lo[:, :, :], in0=y_phase[:, :, :], in1=y_hi[:, :, :].bitcast(F32),
                                  op=ALU.subtract).then_inc(y_split, 1)

            def split_z(t):
                b, p = t.i - 2, t.par(-2)
                dve.wait_ge(z_relaid, RELAY * (b + 1))
                wait(dve, conv3_done, G * (b - 1))
                dve.tensor_copy(z_hi[p][:, :, 1:S + 1], z_tap[:, :, :]).then_inc(z_split, 1)
                dve.wait_ge(z_split, 2 * b + 1)
                dve.tensor_tensor(out=z_lo[p][:, :, 1:S + 1], in0=z_tap[:, :, :],
                                  in1=z_hi[p][:, :, 1:S + 1].bitcast(F32), op=ALU.subtract).then_inc(z_split, 1)

            def mix_matrices(t):
                b, cur = t.i, mix_cur[t.par(0)]
                wait(dve, prod_split, 3 * (b - 1))
                dve.tensor_copy(cur[:, :], mix_tab[:, b, :]).then_inc(cur_done, 1)
                dve.wait_ge(cur_done, b + 1)
                wait(dve, prod_done, b)
                for k in range(K):
                    for l, (w, mat, acc) in enumerate(((mix1_w, mat1, acc1), (mix2_wT, mat2T, acc2))):
                        src, dst = (acc, mat) if k % 2 else (mat, acc)
                        if k:
                            dve.wait_ge(mats_step, 2 * K * b + 2 * (k - 1) + l + 1)
                        dve.scalar_tensor_tensor(out=dst[:, :], in0=w[:, k, :], scalar=cur[:, K * l + k:K * l + k + 1],
                                                 in1=(src if k else ident)[:, :], op0=ALU.mult, op1=ALU.add)\
                           .then_inc(mats_step, 1)

            def split_product(t):
                b = t.i
                dve.wait_ge(prod_done, b + 1)
                wait(dve, mix_done, PH * b)
                dve.tensor_copy(prod_hi[:, :], ps[:, 6, 0:C]).then_inc(prod_split, 1)
                dve.wait_ge(prod_split, 3 * b + 1)
                dve.tensor_tensor(out=prod_lo[:, :], in0=ps[:, 6, 0:C], in1=prod_hi[:, :].bitcast(F32),
                                  op=ALU.subtract).then_inc(prod_split, 1)
                wait(dve, z_evac, 2 * (b - 1))
                dve.tensor_tensor(out=mix_bias[t.par(0)][:, :], in0=ps[:, 6, C:C + 1],
                                  in1=mix_cur[t.par(0)][:, TAB - 1:TAB], op=ALU.add).then_inc(prod_split, 1)

            def one(t):
                if t.has(-2):
                    split_z(t)
                if t.has(0):
                    mix_matrices(t)
                if t.has(1):
                    split_x(t, 1)
                if t.has(0):
                    split_y(t)
                    split_product(t)

            def pad_taps(l, src, dst):
                dve.memset(dst, 0.0).then_inc(padded_step[l], 1)
                dve.wait_ge(conv_w_in[l], DMA)
                dve.wait_ge(padded_step[l], 1)
                dve.tensor_copy(dst[:, :, FIRST:FIRST + TAPS], src).then_inc(padded_step[l], 1)
                if l == 0:
                    dve.wait_ge(ident_step, 2)
                dve.wait_ge(padded_step[l], 2)
                for g in range(G):
                    r = slice(GC * g, GC * g + GC)
                    dve.tensor_tensor(out=dst[r, :, FIRST + PAD], in0=dst[r, :, FIRST + PAD],
                                      in1=ident[r, GC * g:GC * g + GC], op=ALU.add).then_inc(padded_step[l], 1)

            def cut_windows(l, src):
                dve.wait_ge(padded_step[l], 2 + G)
                if l == 1:
                    dve.wait_ge(windows_done[0], JB)
                for j in range(JB):
                    for q in range(PH):
                        a = PH * (j - 1) - q + PAD + FIRST
                        dve.tensor_copy(windows[:, j, q, :].rearrange("o (c p) -> o c p", p=PH), src[:, :, a:a + PH])\
                           .then_inc(windows_cut[l], 1)

            def taps_low(l, hi, lo, order):
                for j in range(JB):
                    dve.wait_ge(taps_hi_done[l], j + 1)
                    dve.tensor_tensor(out=lo[:, j, :, :].rearrange(order, q=PH),
                                      in0=ps[:, j, :].rearrange("r (q g o) -> r g q o", q=PH, g=G),
                                      in1=hi[:, j, :, :].rearrange(order, q=PH).bitcast(F32), op=ALU.subtract)\
                       .then_inc(taps_lo_done[l], 1)

            def bias_columns(l):
                view = "d (g o q) -> d g q o" if l == 0 else "d (g q o) -> d g q o"
                rep = ctx_rep[l].rearrange(view, g=G, q=PH)
                srep = side_rep[l].rearrange(view, g=G, q=PH)
                dve.wait_ge(ctxT_psum[l], 1)
                if l == 0:
                    dve.wait_ge(side_arrived, DMA)
                for q in range(PH):
                    dve.tensor_copy(rep[:, :, q, :], ps[:, 7, 128 * l:128 * l + 128].rearrange("d (g o) -> d g o", g=G))\
                       .then_inc(ctx_rep_done[l], 1)
                    dve.tensor_copy(srep[:, :, q, :], side_in.rearrange("d (g o) -> d g o", g=G))\
                       .then_inc(ctx_rep_done[l], 1)

            def bias_table(l):
                dve.wait_ge(bias_psum[l], 1)
                if l == 0:
                    dve.wait_ge(ident_step, 4)
                dve.tensor_copy(bias_tab[:, 2 * l:2 * l + N, G * l:G * l + G],
                                ps[:, 7, 256 + 128 * l:384 + 128 * l].rearrange("c (g n) -> c n g", g=G))\
                   .then_inc(bias_tab_done[l], 1)

            pad_taps(0, conv0_in, padded0)
            cut_windows(0, padded0)
            dve.wait_ge(condT_psum, 1)
            dve.tensor_copy(condT, ps[:, 6, 0:N]).then_inc(condT_done, 1)
            bias_columns(0)
            taps_low(0, taps0_hi, taps0_lo, "r g (o q) -> r g q o")
            bias_table(0)
            dve.wait_ge(halo_done, HALOS)
            split_x(first, 0)
            pad_taps(1, conv3_in, padded3)
            cut_windows(1, padded3)
            dve.wait_ge(logits_psum, 1)
            for l in range(2):
                dve.tensor_reduce(out=att_max[l], in_=ps[0:N, 6, 192 + K * l:192 + K * l + K], axis=AX.X, op=ALU.max,
                                  negate=True).then_inc(max_done, 1)
            for l in range(2):
                dve.wait_ge(exp_done, l + 1)
                dve.reciprocal(att_inv[l], att_sum[l]).then_inc(att_step, 1)
                dve.wait_ge(att_step, 2 * l + 1)
                dve.tensor_scalar(att[l], att_exp[l], att_inv[l], None, ALU.mult).then_inc(att_step, 1)
            dve.wait_ge(att_step, 4)
            dve.tensor_tensor(out=spread[:, :, :],
                              in0=soft[:, 16:32].rearrange("n (a k) -> n a k", a=1).to_broadcast([N, N, 2 * K]),
                              in1=ident[0:N, 0:N].rearrange("n (m a) -> n m a", a=1).to_broadcast([N, N, 2 * K]),
                              op=ALU.mult).then_inc(spread_done, 1)
            dve.wait_ge(attT_psum, 1)
            dve.tensor_copy(attT_sb[:, :, :], ps[0:K, 6, 256:320].rearrange("k (l n) -> k l n", l=2))\
               .then_inc(attT_done, 1)
            dve.wait_ge(tab_psum, 1)
            dve.tensor_copy(mix_tab[:, :, 0:2 * K], ps[:, 3, :].rearrange("c (n k) -> c n k", n=N))\
               .then_inc(mix_tab_done, 1)
            dve.wait_ge(agg_psum, 1)
            dve.tensor_copy(mix_tab[:, :, 2 * K:TAB], ps[:, 6, 320:384].rearrange("c (l n) -> c n l", l=2))\
               .then_inc(mix_tab_done, 1)
            bias_columns(1)
            taps_low(1, taps3_hi, taps3_lo, "r g (q o) -> r g q o")
            bias_table(1)
            dve.wait_ge(mix_tab_done, 2)
            dve.wait_ge(mix1_arrived, DMA)
            dve.wait_ge(mix2T_done, 2)
            steps(dve, one)

        @block.tensor
        def _(pe):
            def conv_tile(g, bank, hi, lo, w_hi, w_lo, done):
                n = 0
                for j in range(JB):
                    for w, a in ((w_hi, hi), (w_hi, lo), (w_lo, hi)):
                        last = pe.matmul(ps[:, bank, :], w[:, j, g, :], a[:, g, j:j + S], start=(n == 0),
                                         stop=(n == 3 * JB - 1))
                        n += 1
                last.then_inc(done, 1)

            def conv0_tile(t, g):
                b = t.i
                if g == 0:
                    pe.wait_ge(x_split, 2 * b + 2)
                    wait(pe, z_evac, 2 * (b - 1))
                if g == 2:
                    wait(pe, out_evac, G * PH * (b - 3) + 2 * PH)
                conv_tile(g, g, x_hi[t.par(0)], x_lo[t.par(0)], taps0_hi, taps0_lo, conv0_done)

            def mix(t):
                b = t.i - 1
                pe.wait_ge(y_split, 2 * b + 2)
                pe.wait_ge(prod_split, 3 * b + 2)
                for q in range(PH):
                    bank = (4, 5, 0, 1)[q]
                    if q == 0:
                        wait(pe, out_evac, G * PH * (b - 1))
                    if q == 2 and t.has(0):
                        pe.wait_ge(y_evac, G * t.i + 2)
                    for n, (w, a) in enumerate(((prod_hi, y_hi), (prod_hi, y_lo), (prod_lo, y_hi))):
                        last = pe.matmul(ps[:, bank, :], w[:, :], a[:, q, :], start=(n == 0), stop=(n == 2))
                    last.then_inc(mix_done, 1)

            def product(t):
                b = t.i
                pe.wait_ge(mats_step, 2 * K * (b + 1))
                wait(pe, prod_split, 3 * b)
                pe.matmul(ps[:, 6, 0:C], mat1[:, :], mat2T[:, :], start=True, stop=True)
                pe.matmul(ps[:, 6, C:C + 1], mat2T[:, :], mix_cur[t.par(0)][:, 2 * K:2 * K + 1], start=True, stop=True)\
                  .then_inc(prod_done, 1)

            def conv3(t):
                b = t.i - 2
                pe.wait_ge(z_split, 2 * b + 2)
                for g in range(G):
                    if g == 0 and t.has(0):
                        pe.wait_ge(y_evac, G * t.i + 4)
                    if g == 0 and not t.has(0):
                        wait(pe, out_evac, G * PH * b)
                    if g == 2 and t.has(-1):
                        pe.wait_ge(z_evac, 2 * (b + 1) + 1)
                    conv_tile(g, 2 + g, z_hi[t.par(0)], z_lo[t.par(0)], taps3_hi, taps3_lo, conv3_done)

            def one(t):
                if t.has(0) and t is not first:
                    for g in range(G):
                        conv0_tile(t, g)
                if t.has(-1):
                    mix(t)
                if t.has(0):
                    product(t)
                if t.has(-2):
                    conv3(t)

            def tap_windows(l):
                for j in range(JB):
                    pe.wait_ge(windows_cut[l], PH * (j + 1))
                    if l == 1:
                        pe.wait_ge(y_evac, min(j + 1, G))
                    for q in range(PH):
                        last = pe.transpose(ps[:, j, 128 * q:128 * q + 128], windows[:, j, q, :], ident[:, :])
                    last.then_inc(windows_done[l], 1)

            def conv_bias(l):
                pe.wait_ge(ctx_rep_done[l], 2 * PH)
                for g in range(G):
                    o = ps[:, 7, 256 + 128 * l + N * g:256 + 128 * l + N * g + N]
                    pe.matmul(o, ctx_rep[l][:, 128 * g:128 * g + 128], condT, start=True, stop=False)
                    last = pe.matmul(o, side_rep[l][:, 128 * g:128 * g + 128], ones[0:1, 0:N], start=False, stop=True)
                last.then_inc(bias_psum[l], 1)

            def hidden(m):
                if m == 0:
                    pe.wait_ge(mlp_arrived, 14 * DMA)
                else:
                    pe.wait_ge(hidden_done, 2)
                for l in range(2):
                    at = 64 + 32 * (2 * m + l)
                    last = pe.matmul(ps[:, 6, at:at + 32], mlp_w[l][m], condT if m == 0 else hid[l][0],
                                     start=True, stop=True)
                last.then_inc(hidden_psum, 1)

            def logits():
                pe.wait_ge(hidden_done, 4)
                for l in range(2):
                    o = ps[0:N, 6, 192 + K * l:192 + K * l + K]
                    pe.matmul(o, hid[l][1], key_w[l], start=True, stop=False)
                    last = pe.matmul(o, ones[0:1, 0:N], key_b[l], start=False, stop=True)
                last.then_inc(logits_psum, 1)

            pe.wait_ge(ident_step, 3)
            pe.wait_ge(cond_arrived, DMA)
            pe.transpose(ps[:, 6, 0:N], cond_in, ident[0:N, 0:N]).then_inc(condT_psum, 1)
            pe.wait_ge(ctx_w_in[0], DMA)
            pe.transpose(ps[:, 7, 0:128], ctx_in[0], ident[:, :]).then_inc(ctxT_psum[0], 1)
            tap_windows(0)
            pe.wait_ge(condT_done, 1)
            conv_bias(0)
            pe.wait_ge(taps_hi_done[0], JB)
            pe.wait_ge(taps_lo_done[0], JB)
            pe.wait_ge(halo_done, HALOS)
            hidden(0)
            conv0_tile(first, 0)
            hidden(1)
            conv0_tile(first, 1)
            logits()
            conv0_tile(first, 2)
            pe.wait_ge(mix2_arrived, DMA)
            for h in range(2):
                for k in range(4):
                    last = pe.transpose(ps[:, 4 + h, 128 * k:128 * k + 128], mix2_in[:, 4 * h + k, :], ident[:, :])
                last.then_inc(mix2T_psum, 1)
            conv0_tile(first, 3)
            pe.wait_ge(ctx_w_in[1], DMA)
            pe.wait_ge(bias_tab_done[0], 1)
            pe.transpose(ps[:, 7, 128:256], ctx_in[1], ident[:, :]).then_inc(ctxT_psum[1], 1)
            pe.wait_ge(att_step, 4)
            for l in range(2):
                last = pe.transpose(ps[0:K, 6, 256 + N * l:256 + N * l + N], att[l], ident[0:N, 0:N])
            last.then_inc(attT_psum, 1)
            pe.wait_ge(spread_done, 1)
            pe.wait_ge(y_evac, G)
            pe.matmul(ps[:, 3, :], ones[0:N, :], spread[:, :, :].rearrange("n m k -> n (m k)"), start=True, stop=True)\
              .then_inc(tab_psum, 1)
            pe.wait_ge(attT_done, 1)
            for l in range(2):
                last = pe.matmul(ps[:, 6, 320 + N * l:320 + N * l + N], bias_k[l], attT_sb[:, l, :], start=True, stop=True)
            last.then_inc(agg_psum, 1)
            tap_windows(1)
            conv_bias(1)
            pe.wait_ge(taps_hi_done[1], JB)
            pe.wait_ge(taps_lo_done[1], JB)
            pe.wait_ge(mix_tab_done, 2)
            pe.wait_ge(bias_tab_done[1], 1)
            steps(pe, one)


_INS = ['x', 'cond_128', 'fside_S_0', 'L0_cond_weight', 'L0_cond_c_weight',
        'L1_cond_W0', 'L1_cond_b0', 'L1_cond_W1', 'L1_cond_b1', 'L1_cond_W2', 'L1_cond_b2', 'L1_cond_weight',
        'L1_cond_bias_k', 'L2_cond_W0', 'L2_cond_b0', 'L2_cond_W1', 'L2_cond_b1', 'L2_cond_W2', 'L2_cond_b2',
        'L2_cond_weight', 'L2_cond_bias_k', 'L3_cond_weight', 'L3_cond_c_weight']


def kernel(**inputs):
    import numpy as _np
    import concourse.bacc as _bacc
    from concourse import mybir as _mybir
    from concourse.bass_utils import run_bass_kernel_spmd as _run

    nc = _bacc.Bacc("TRN2", target_bir_lowering=False, num_devices=1)
    arrays, a = {}, {}
    for name in _INS:
        v = _np.ascontiguousarray(inputs[name])
        if v.ndim == 4:
            v = v.reshape(v.shape[:3])
        arrays[f"in_{name}"] = v
        a[name] = nc.dram_tensor(f"in_{name}", v.shape, _mybir.dt.from_np(v.dtype), kind="ExternalInput").ap()
    out = nc.dram_tensor("out", (N, C, L), F32, kind="ExternalOutput").ap()
    mixes = [[a[f"L{l}_cond_{n}"] for n in ("W0", "b0", "W1", "b1", "W2", "b2", "weight", "bias_k")] for l in (1, 2)]
    conditioned_residual_kernel(nc, a['x'], a['cond_128'], a['fside_S_0'], a['L0_cond_weight'], a['L0_cond_c_weight'],
                                mixes[0], mixes[1], a['L3_cond_weight'], a['L3_cond_c_weight'], out)
    r = _run(nc, [arrays], core_ids=[0])
    return r.results[0]["out"]
```

```python
from contextlib import ExitStack

import concourse.bass as bass
from concourse import mybir

F32 = mybir.dt.float32
F32R = mybir.dt.float32r
ALU = mybir.AluOpType
ACT = mybir.ActivationFunctionType
AX = mybir.AxisListType

N, C, L = 32, 128, 2048
G = 4
GC = C // G
TAPS, PAD = 9, 4
PH = C // GC
S = L // PH
JB = 3
SLOTS = PH * JB + PH - 1
FIRST = PH - 1
K = 8
D = 128
DMA = 16
RELAY = G * DMA
ATT = 2 * K
BIAS = 2 * G + 1


def conditioned_residual_kernel(nc, x, cond, side, conv0_w, ctx0_w, mix1, mix2, conv3_w, ctx3_w, out):
    ctx = ExitStack()
    with ctx:
        def sb(name, shape, dt=F32):
            return ctx.enter_context(nc.sbuf_tensor(name, shape, dt))

        def sem(name):
            return ctx.enter_context(nc.semaphore(name))

        x_in = [sb(f"x_in{i}", [C, L]) for i in range(2)]
        x_phase = sb("x_phase", [C, PH, S])
        x_tap = sb("x_tap", [C, G, S])
        x_hi = [sb(f"x_hi{i}", [C, G, S + 2], F32R) for i in range(2)]
        x_lo = [sb(f"x_lo{i}", [C, G, S + 2], F32R) for i in range(2)]
        y_tap = sb("y_tap", [C, G, S])
        y_phase = sb("y_phase", [C, PH, S])
        y_hi = sb("y_hi", [C, PH, S], F32R)
        y_lo = sb("y_lo", [C, PH, S], F32R)
        z_phase = sb("z_phase", [C, PH, S])
        z_tap = sb("z_tap", [C, G, S])
        z_hi = [sb(f"z_hi{i}", [C, G, S + 2], F32R) for i in range(2)]
        z_lo = [sb(f"z_lo{i}", [C, G, S + 2], F32R) for i in range(2)]
        out_sb = [sb(f"out_sb{i}", [C, L]) for i in range(2)]

        taps0_hi = sb("taps0_hi", [C, JB, G, C], F32R)
        taps0_lo = sb("taps0_lo", [C, JB, G, C], F32R)
        taps3_hi = sb("taps3_hi", [C, JB, G, C], F32R)
        taps3_lo = sb("taps3_lo", [C, JB, G, C], F32R)
        mix1_w = sb("mix1_w", [C, K, C])
        mix2_wT = sb("mix2_wT", [C, K, C])
        mat1 = sb("mat1", [C, C])
        mat2T = sb("mat2T", [C, C])
        acc1 = sb("acc1", [C, C])
        acc2 = sb("acc2", [C, C])
        prod_hi = sb("prod_hi", [C, C], F32R)
        prod_lo = sb("prod_lo", [C, C], F32R)
        att_tab = sb("att_tab", [C, N, ATT])
        att_cur = [sb(f"att_cur{i}", [C, ATT]) for i in range(2)]
        agg = sb("agg", [C, 2, N])
        bias_tab = sb("bias_tab", [C, N + 2, BIAS])
        bias_cur = [sb(f"bias_cur{i}", [C, BIAS]) for i in range(2)]
        ident = sb("ident", [C, C])
        ones = sb("ones", [GC, C])

        o0, o1 = out_sb[0], out_sb[1]
        padded0 = o0[:, 0:GC * SLOTS].rearrange("o (c k) -> o c k", k=SLOTS)
        conv0_in = o0[:, 480:480 + GC * TAPS].rearrange("o (c k) -> o c k", k=TAPS)
        padded3 = o0[:, 768:768 + GC * SLOTS].rearrange("o (c k) -> o c k", k=SLOTS)
        conv3_in = o0[:, 1248:1248 + GC * TAPS].rearrange("o (c k) -> o c k", k=TAPS)
        side_rep = [o0[0:1, 1536:2048], z_phase[0:1, 3, :]]
        windows = [b[:, :, :].rearrange("c p s -> c (p s)")[:, 0:JB * PH * C]
                   .rearrange("o (j q m) -> o j q m", j=JB, q=PH) for b in (z_phase, z_tap)]
        z3 = z_tap[:, 3, :]
        ctx_in = [z3[:, 128 * l:128 * l + 128] for l in range(2)]
        condT = z3[:, 256:256 + N]
        cond_in = z3[0:N, 288:416]
        ctx_rep = [o1[:, 512 * l:512 * l + 512] for l in range(2)]
        side_in = sb("side_in", [1, C])[:, :]
        mlp_w = [[o1[:, 1024 + 256 * l + 128 * m:1152 + 256 * l + 128 * m] for m in range(2)] for l in range(2)]
        mlp_b = [[o1[:, 1536 + 2 * l + m:1537 + 2 * l + m] for m in range(2)] for l in range(2)]
        key_w = [o1[:, 1544 + K * l:1544 + K * l + K] for l in range(2)]
        key_b = [o1[0:1, 1560 + K * l:1560 + K * l + K] for l in range(2)]
        bias_k = [o1[0:K, 1576 + 128 * l:1704 + 128 * l] for l in range(2)]
        hid = [[o1[:, 1832 + 32 * (2 * l + m):1864 + 32 * (2 * l + m)] for m in range(2)] for l in range(2)]
        mixed_terms = o0[:, 0:N * K].rearrange("c (n k) -> c n k", k=K)
        mixed_sum = o0[:, 480:480 + N]
        soft = sb("soft", [N, 64])
        att_exp = [soft[:, K * l:K * l + K] for l in range(2)]
        att = [soft[:, 16 + K * l:16 + K * l + K] for l in range(2)]
        att_max = [soft[:, 32 + l:33 + l] for l in range(2)]
        att_sum = [soft[:, 34 + l:35 + l] for l in range(2)]
        att_inv = [soft[:, 36 + l:37 + l] for l in range(2)]
        attT_sb = sb("attT_sb", [K, 2, N])
        spread = sb("spread", [N, N, 2 * K])
        mix2_in = y_phase[:, :, :].rearrange("c p s -> c (p s)")[:, 0:K * C].rearrange("o (k i) -> o k i", i=C)

        ps = ctx.enter_context(nc.psum_tensor("ps", [C, 8, 512], F32))

        conv_w_in = [sem(f"conv_w_in{l}") for l in range(2)]
        ctx_w_in = [sem(f"ctx_w_in{l}") for l in range(2)]
        cond_arrived = sem("cond_arrived")
        side_arrived = sem("side_arrived")
        mlp_w_arrived = sem("mlp_w_arrived")
        mlp_arrived = sem("mlp_arrived")
        mix1_arrived = sem("mix1_arrived")
        mix2_arrived = sem("mix2_arrived")
        ident_step = sem("ident_step")
        padded_step = [sem(f"padded_step{l}") for l in range(2)]
        windows_cut = [sem(f"windows_cut{l}") for l in range(2)]
        windows_done = [sem(f"windows_done{l}") for l in range(2)]
        taps_hi_done = [sem(f"taps_hi_done{l}") for l in range(2)]
        taps_lo_done = [sem(f"taps_lo_done{l}") for l in range(2)]
        condT_psum = sem("condT_psum")
        condT_done = sem("condT_done")
        ctxT_psum = [sem(f"ctxT_psum{l}") for l in range(2)]
        ctx_rep_done = [sem(f"ctx_rep_done{l}") for l in range(2)]
        bias_psum = [sem(f"bias_psum{l}") for l in range(2)]
        bias_tab_done = sem("bias_tab_done")
        hidden_psum = sem("hidden_psum")
        hidden_done = sem("hidden_done")
        logits_psum = sem("logits_psum")
        max_done = sem("max_done")
        exp_done = sem("exp_done")
        att_step = sem("att_step")
        spread_done = sem("spread_done")
        attT_psum = sem("attT_psum")
        attT_done = sem("attT_done")
        att_tab_psum = sem("att_tab_psum")
        att_tab_done = sem("att_tab_done")
        agg_psum = sem("agg_psum")
        agg_done = sem("agg_done")
        mixed_psum = sem("mixed_psum")
        mixed_step = sem("mixed_step")
        mix2T_psum = sem("mix2T_psum")
        mix2T_done = sem("mix2T_done")
        halo_done = sem("halo_done")

        x_loaded = [sem(f"x_loaded{i}") for i in range(2)]
        x_phased = sem("x_phased")
        x_relaid = sem("x_relaid")
        x_split = sem("x_split")
        conv0_done = sem("conv0_done")
        y_evac = sem("y_evac")
        y_relaid = sem("y_relaid")
        y_split = sem("y_split")
        mats_step = sem("mats_step")
        cur_done = sem("cur_done")
        prod_done = sem("prod_done")
        prod_split = sem("prod_split")
        mix_done = sem("mix_done")
        z_evac = sem("z_evac")
        z_relaid = sem("z_relaid")
        z_split = sem("z_split")
        conv3_done = sem("conv3_done")
        bias_done = sem("bias_done")
        out_evac = sem("out_evac")
        out_stored = [sem(f"out_stored{i}") for i in range(2)]

        block = ctx.enter_context(nc.Block())

        def wait(eng, s, value):
            if not isinstance(value, int) or value > 0:
                eng.wait_ge(s, value)

        class Step:

            def __init__(self, half, parity):
                self.half, self.parity, self.i = half, parity, 2 * half + parity

            def has(self, d):
                return not isinstance(self.half, int) or 0 <= self.i + d < N

            def at(self, i):
                return isinstance(self.half, int) and self.i == i

            def par(self, d):
                return (self.parity + d) % 2

            def pair(self, d):
                return self.half + (self.parity + d) // 2

        LOOP = (2, (N - 4) // 2)

        def steps(eng, one):
            for i in range(2 * LOOP[0]):
                one(Step(i // 2, i % 2) if i else first)
            with eng.Fori(LOOP[0], LOOP[1]) as half:
                one(Step(half, 0))
                one(Step(half, 1))
            for i in range(2 * LOOP[1], N + 2):
                one(Step(i // 2, i % 2))

        first = Step(0, 0)

        def window_bank(l, j):
            return (j, (4, 5, 7)[j])[l]

        def x_splits(b):
            return 2 * (b + G)

        @block.sync
        def _(sp):
            def count(value):
                return value if isinstance(value, int) else sp.snap(sp.to_reg(value))

            def load_x(t, d):
                b, read = count(t.i + d), count(t.i + d - 1)
                src = x[b]
                wait(sp, x_phased, read)
                sp.dma_start(x_in[t.par(d)][:, :], src).then_inc(x_loaded[t.par(d)], DMA)

            def relay_x(t, d):
                b = t.i + d
                written, read = count(b + 1), 0 if t is first and d == 0 else count(x_splits(b - 1))
                wait(sp, x_split, read)
                wait(sp, x_phased, written)
                for g in range(G):
                    sp.dma_start(x_tap[:, g, :], x_phase[GC * g:GC * g + GC, :, :]).then_inc(x_relaid, DMA)

            def relay_y(t):
                read, written = count(2 * t.i), [count(G * t.i + g + 1) for g in range(G)]
                wait(sp, y_split, read)
                for g in range(G):
                    wait(sp, y_evac, written[g])
                    sp.dma_start(y_phase[GC * g:GC * g + GC, :, :], y_tap[:, g, :]).then_inc(y_relaid, DMA)

            def relay_z(t):
                written, read = count(2 * t.i), count(2 * (t.i - 1))
                wait(sp, z_evac, written)
                wait(sp, z_split, read)
                for g in range(G):
                    sp.dma_start(z_tap[:, g, :], z_phase[GC * g:GC * g + GC, :, :]).then_inc(z_relaid, DMA)

            def store(t):
                b, written = count(t.i - 3), count(G * PH * (t.i - 2))
                dst = out[b]
                wait(sp, out_evac, written)
                sp.dma_start(dst, out_sb[t.par(-3)][:, :]).then_inc(out_stored[t.par(-3)], DMA)

            def one(t):
                if t.has(1):
                    relay_x(t, 1)
                if t.has(3):
                    load_x(t, 3)
                if t.has(-3):
                    store(t)
                if t.has(0):
                    relay_y(t)
                if t.has(-1):
                    relay_z(t)

            sp.dma_start(conv0_in, conv0_w).then_inc(conv_w_in[0], DMA)
            load_x(first, 0)
            load_x(first, 1)
            relay_x(first, 0)
            load_x(first, 2)
            sp.dma_start(mix1_w[:, :, :], mix1[6].rearrange("k o i -> o k i")).then_inc(mix1_arrived, DMA)
            sp.wait_ge(mix2T_psum, 2)
            steps(sp, one)
            b = N - 1
            for g in range(G):
                sp.wait_ge(out_evac, G * PH * b + PH * (g + 1))
                sp.dma_start(out[b, GC * g:GC * g + GC, :], out_sb[b % 2][GC * g:GC * g + GC, :])\
                  .then_inc(out_stored[b % 2], DMA)
            sp.wait_ge(out_stored[0], DMA * (N // 2))
            sp.wait_ge(out_stored[1], DMA * (N // 2 - 1 + G))

        def pad_taps(eng, l, src, dst):
            eng.memset(dst, 0.0).then_inc(padded_step[l], 1)
            eng.wait_ge(conv_w_in[l], DMA)
            eng.wait_ge(padded_step[l], 1)
            eng.tensor_copy(dst[:, :, FIRST:FIRST + TAPS], src).then_inc(padded_step[l], 1)
            eng.wait_ge(ident_step, 2)
            eng.wait_ge(padded_step[l], 2)
            for g in range(G):
                r = slice(GC * g, GC * g + GC)
                eng.tensor_tensor(out=dst[r, :, FIRST + PAD], in0=dst[r, :, FIRST + PAD],
                                  in1=ident[r, GC * g:GC * g + GC], op=ALU.add).then_inc(padded_step[l], 1)

        def cut_windows(eng, l, src):
            eng.wait_ge(padded_step[l], 2 + G)
            for j in range(JB):
                for q in range(PH):
                    a = PH * (j - 1) - q + PAD + FIRST
                    eng.tensor_copy(windows[l][:, j, q, :].rearrange("o (c p) -> o c p", p=PH), src[:, :, a:a + PH])\
                       .then_inc(windows_cut[l], 1)

        @block.gpsimd
        def _(pool):
            pool.memset(ident[:, :], 0.0).then_inc(ident_step, 1)
            pool.wait_ge(ident_step, 1)
            pool.affine_select(out=ident[:, :], in_=ident[:, :], compare_op=ALU.not_equal, fill=1.0, base=0,
                               pattern=[[-1, C]], channel_multiplier=1).then_inc(ident_step, 1)
            pool.memset(ones[:, :], 1.0).then_inc(ident_step, 1)
            pool.memset(bias_tab[:, :, :], 0.0).then_inc(ident_step, 1)
            for l, m in enumerate((mix1, mix2)):
                pool.dma_start(mlp_b[l][0], m[1].rearrange("(c a) -> c a", a=1)).then_inc(mlp_arrived, DMA)
                pool.dma_start(mlp_b[l][1], m[3].rearrange("(c a) -> c a", a=1)).then_inc(mlp_arrived, DMA)
                pool.dma_start(key_w[l], m[4]).then_inc(mlp_arrived, DMA)
                pool.dma_start(key_b[l], m[5].rearrange("(a k) -> a k", a=1)).then_inc(mlp_arrived, DMA)
                pool.dma_start(bias_k[l], m[7]).then_inc(mlp_arrived, DMA)
            for buf in x_hi + x_lo + z_hi + z_lo:
                pool.memset(buf[:, :, 0:S + 2:S + 1].bitcast(F32), 0.0).then_inc(halo_done, 1)
            pad_taps(pool, 1, conv3_in, padded3)
            cut_windows(pool, 1, padded3)

        HALOS = 8

        @block.scalar
        def _(act):
            def phase_x(t, d):
                b = t.i + d
                act.wait_ge(x_loaded[t.par(d)], DMA * (t.pair(d) + 1))
                wait(act, x_relaid, RELAY * b)
                act.activation(x_phase[:, :, :], x_in[t.par(d)][:, :].rearrange("c (s p) -> c p s", p=PH),
                               ACT.Copy).then_inc(x_phased, 1)

            def copy_bias(t):
                wait(act, y_evac, G * (t.i - 1))
                wait(act, z_evac, 2 * (t.i - 2))
                wait(act, out_evac, G * PH * (t.i - 3))
                act.activation(bias_cur[t.par(0)][:, :], bias_tab[:, t.i, :], ACT.Copy).then_inc(bias_done, 1)

            def evac_y(t, g):
                b = t.i
                if g == 0:
                    act.wait_ge(bias_done, b + 1)
                    wait(act, y_relaid, RELAY * b)
                act.wait_ge(conv0_done, G * b + g + 1)
                act.activation(y_tap[:, g, :], ps[:, g, :], ACT.Identity,
                               bias=bias_cur[t.par(0)][:, g:g + 1]).then_inc(y_evac, 1)

            def evac_z(t):
                b = t.i - 1
                act.wait_ge(bias_done, t.i + 1)
                wait(act, z_relaid, RELAY * b)
                for h in range(2):
                    act.wait_ge(mix_done, PH * b + 2 * h + 2)
                    bank = 4 if h == 0 else 0
                    act.activation(z_phase[:, 2 * h:2 * h + 2, :], ps[:, bank:bank + 2, :], ACT.Identity,
                                   bias=bias_cur[t.par(0)][:, 2 * G:BIAS]).then_inc(z_evac, 1)

            def evac_out(t):
                b = t.i - 2
                act.wait_ge(bias_done, t.i + 1)
                wait(act, out_stored[t.par(0)], DMA * t.pair(-2))
                o = out_sb[t.par(0)][:, :].rearrange("c (s p) -> c p s", p=PH)
                for g in range(G):
                    act.wait_ge(conv3_done, G * b + g + 1)
                    for q in range(PH):
                        act.activation(o[GC * g:GC * g + GC, q, :], ps[GC * q:GC * q + GC, 2 + g, :], ACT.Identity,
                                       bias=bias_cur[t.par(0)][GC * q:GC * q + GC, G + g:G + g + 1])\
                           .then_inc(out_evac, 1)

            def taps_high(l, j):
                hi, view = ((taps0_hi, "r g (o q) -> r g q o"), (taps3_hi, "r g (q o) -> r g q o"))[l]
                act.wait_ge(windows_done[l], j + 1)
                act.activation(hi[:, j, :, :].rearrange(view, q=PH),
                               ps[:, window_bank(l, j), :].rearrange("r (q g o) -> r g q o", q=PH, g=G), ACT.Copy)\
                   .then_inc(taps_hi_done[l], 1)

            def gelus(m):
                act.wait_ge(hidden_psum, m + 1)
                for l in range(2):
                    act.activation(hid[l][m], ps[:, 6, 64 + 32 * (2 * m + l):96 + 32 * (2 * m + l)], ACT.Gelu,
                                   bias=mlp_b[l][m]).then_inc(hidden_done, 1)

            def one(t):
                if t is not first:
                    copy_bias(t)
                    for g in range(G):
                        if t.has(0):
                            evac_y(t, g)
                        if g == 1 and t.has(2):
                            phase_x(t, 2)
                        if g < JB and t.at(1):
                            taps_high(1, g)
                if t.has(-1):
                    evac_z(t)
                if t.has(-2):
                    evac_out(t)

            act.dma_start(cond_in, cond).then_inc(cond_arrived, DMA)
            act.dma_start(ctx_in[0], ctx0_w).then_inc(ctx_w_in[0], DMA)
            act.dma_start(side_in, side.rearrange("(a c) -> a c", a=1)).then_inc(side_arrived, DMA)
            act.dma_start(mlp_w[0][0], mix1[0]).then_inc(mlp_w_arrived, DMA)
            act.dma_start(mlp_w[1][0], mix2[0]).then_inc(mlp_w_arrived, DMA)
            phase_x(first, 0)
            act.dma_start(ctx_in[1], ctx3_w).then_inc(ctx_w_in[1], DMA)
            act.dma_start(mlp_w[0][1], mix1[2]).then_inc(mlp_w_arrived, DMA)
            act.dma_start(mlp_w[1][1], mix2[2]).then_inc(mlp_w_arrived, DMA)
            act.dma_start(mix2_in, mix2[6].rearrange("k o i -> o k i")).then_inc(mix2_arrived, DMA)
            act.dma_start(conv3_in, conv3_w).then_inc(conv_w_in[1], DMA)
            for j in range(JB):
                taps_high(0, j)
            gelus(0)
            phase_x(first, 1)
            gelus(1)
            act.wait_ge(bias_tab_done, 2)
            copy_bias(first)
            evac_y(first, 0)
            act.wait_ge(max_done, 2)
            for l in range(2):
                act.activation(att_exp[l], ps[0:N, 6, 192 + K * l:192 + K * l + K], ACT.Exp,
                               bias=att_max[l], accum_out=att_sum[l]).then_inc(exp_done, 1)
            evac_y(first, 1)
            evac_y(first, 2)
            for h in range(2):
                act.wait_ge(mix2T_psum, h + 1)
                act.activation(mix2_wT[:, 4 * h:4 * h + 4, :].rearrange("i k o -> i (k o)"), ps[:, 4 + h, :],
                               ACT.Copy).then_inc(mix2T_done, 1)
            evac_y(first, 3)
            phase_x(first, 2)
            act.wait_ge(bias_tab_done, 3)
            steps(act, one)

        @block.vector
        def _(dve):
            def split(done, before, hi, lo, src):
                dve.tensor_copy(hi, src).then_inc(done, 1)
                dve.wait_ge(done, before + 1)
                dve.tensor_tensor(out=lo, in0=src, in1=hi.bitcast(F32), op=ALU.subtract).then_inc(done, 1)

            def split_x(t, d):
                b, p = t.i + d, t.par(d)
                dve.wait_ge(x_relaid, RELAY * (b + 1))
                wait(dve, conv0_done, G * (b - 1))
                split(x_split, x_splits(b - 1), x_hi[p][:, :, 1:S + 1], x_lo[p][:, :, 1:S + 1], x_tap[:, :, :])

            def split_y(t):
                b = t.i
                dve.wait_ge(y_relaid, RELAY * (b + 1))
                wait(dve, mix_done, PH * b)
                split(y_split, 2 * b, y_hi[:, :, :], y_lo[:, :, :], y_phase[:, :, :])

            def split_z(t):
                b, p = t.i - 2, t.par(-2)
                dve.wait_ge(z_relaid, RELAY * (b + 1))
                wait(dve, conv3_done, G * (b - 1))
                split(z_split, 2 * b, z_hi[p][:, :, 1:S + 1], z_lo[p][:, :, 1:S + 1], z_tap[:, :, :])

            def mix_matrices(t):
                b, cur = t.i, att_cur[t.par(0)]
                dve.tensor_copy(cur[:, :], att_tab[:, b, :]).then_inc(cur_done, 1)
                dve.wait_ge(cur_done, b + 1)
                wait(dve, prod_done, b)
                for k in range(K):
                    for l, (w, mat, acc) in enumerate(((mix1_w, mat1, acc1), (mix2_wT, mat2T, acc2))):
                        src, dst = (acc, mat) if k % 2 else (mat, acc)
                        if k:
                            dve.wait_ge(mats_step, 2 * K * b + 2 * (k - 1) + l + 1)
                        dve.scalar_tensor_tensor(out=dst[:, :], in0=w[:, k, :], scalar=cur[:, K * l + k:K * l + k + 1],
                                                 in1=(src if k else ident)[:, :], op0=ALU.mult, op1=ALU.add)\
                           .then_inc(mats_step, 1)

            def split_product(t):
                b = t.i - 1
                dve.wait_ge(prod_done, b + 1)
                wait(dve, mix_done, PH * b)
                split(prod_split, 2 * b, prod_hi[:, :], prod_lo[:, :], ps[:, 6, 0:C])

            def one(t):
                if t.has(-1) and not t.has(0):
                    split_product(t)
                if t.has(-2) and not t.at(N + 1):
                    split_z(t)
                if t.has(1):
                    split_x(t, 1)
                if t.has(-1) and t.has(0):
                    split_product(t)
                if t.at(1):
                    taps_low(1)
                if t.has(0):
                    mix_matrices(t)
                    split_y(t)

            def taps_low(l):
                hi, lo, view = ((taps0_hi, taps0_lo, "r g (o q) -> r g q o"),
                                (taps3_hi, taps3_lo, "r g (q o) -> r g q o"))[l]
                for j in range(JB):
                    dve.wait_ge(taps_hi_done[l], j + 1)
                    dve.tensor_tensor(out=lo[:, j, :, :].rearrange(view, q=PH),
                                      in0=ps[:, window_bank(l, j), :].rearrange("r (q g o) -> r g q o", q=PH, g=G),
                                      in1=hi[:, j, :, :].rearrange(view, q=PH).bitcast(F32), op=ALU.subtract)\
                       .then_inc(taps_lo_done[l], 1)

            def bias_columns(l):
                view = "d (g o q) -> d g q o" if l == 0 else "d (g q o) -> d g q o"
                rep = ctx_rep[l].rearrange(view, g=G, q=PH)
                srep = side_rep[l].rearrange(view, g=G, q=PH)
                dve.wait_ge(ctxT_psum[l], 1)
                dve.wait_ge(side_arrived, DMA)
                for q in range(PH):
                    dve.tensor_copy(rep[:, :, q, :], ps[:, 7, 128 * l:128 * l + 128].rearrange("d (g o) -> d g o", g=G))\
                       .then_inc(ctx_rep_done[l], 1)
                    dve.tensor_copy(srep[:, :, q, :], side_in.rearrange("d (g o) -> d g o", g=G))\
                       .then_inc(ctx_rep_done[l], 1)

            def bias_table(l):
                dve.wait_ge(bias_psum[l], 1)
                dve.wait_ge(ident_step, 4)
                dve.tensor_copy(bias_tab[:, 2 * l:2 * l + N, G * l:G * l + G],
                                ps[:, 7, 256 + 128 * l:384 + 128 * l].rearrange("c (g n) -> c n g", g=G))\
                   .then_inc(bias_tab_done, 1)

            pad_taps(dve, 0, conv0_in, padded0)
            cut_windows(dve, 0, padded0)
            dve.wait_ge(condT_psum, 1)
            dve.tensor_copy(condT, ps[:, 6, 0:N]).then_inc(condT_done, 1)
            dve.wait_ge(halo_done, HALOS)
            taps_low(0)
            for g in range(G):
                dve.wait_ge(x_relaid, RELAY)
                split(x_split, 2 * g, x_hi[0][:, g, 1:S + 1], x_lo[0][:, g, 1:S + 1], x_tap[:, g, :])
            bias_columns(0)
            bias_table(0)
            dve.wait_ge(logits_psum, 1)
            for l in range(2):
                dve.tensor_reduce(out=att_max[l], in_=ps[0:N, 6, 192 + K * l:192 + K * l + K], axis=AX.X, op=ALU.max,
                                  negate=True).then_inc(max_done, 1)
            bias_columns(1)
            bias_table(1)
            for l in range(2):
                dve.wait_ge(exp_done, l + 1)
                dve.reciprocal(att_inv[l], att_sum[l]).then_inc(att_step, 1)
                dve.wait_ge(att_step, 2 * l + 1)
                dve.tensor_scalar(att[l], att_exp[l], att_inv[l], None, ALU.mult).then_inc(att_step, 1)
            dve.wait_ge(att_step, 4)
            dve.tensor_tensor(out=spread[:, :, :],
                              in0=soft[:, 16:32].rearrange("n (a k) -> n a k", a=1).to_broadcast([N, N, 2 * K]),
                              in1=ident[0:N, 0:N].rearrange("n (m a) -> n m a", a=1).to_broadcast([N, N, 2 * K]),
                              op=ALU.mult).then_inc(spread_done, 1)
            dve.wait_ge(attT_psum, 1)
            dve.tensor_copy(attT_sb[:, :, :], ps[0:K, 6, 256:320].rearrange("k (l n) -> k l n", l=2))\
               .then_inc(attT_done, 1)
            split_x(first, 1)
            dve.wait_ge(att_tab_psum, 1)
            dve.tensor_copy(att_tab[:, :, :], ps[:, 0, :].rearrange("c (n k) -> c n k", n=N)).then_inc(att_tab_done, 1)
            dve.wait_ge(agg_psum, 1)
            dve.tensor_copy(agg[:, :, :], ps[:, 6, 320:384].rearrange("c (l n) -> c l n", l=2)).then_inc(agg_done, 1)
            dve.wait_ge(mixed_psum, 1)
            dve.wait_ge(att_tab_done, 1)
            dve.tensor_tensor(out=mixed_terms, in0=ps[:, 7, 0:N * K].rearrange("c (k n) -> c n k", k=K),
                              in1=att_tab[:, :, K:2 * K], op=ALU.mult).then_inc(mixed_step, 1)
            dve.wait_ge(mixed_step, 1)
            dve.tensor_reduce(out=mixed_sum, in_=mixed_terms, axis=AX.X, op=ALU.add).then_inc(mixed_step, 1)
            dve.wait_ge(agg_done, 1)
            for l in range(2):
                dve.wait_ge(mixed_step, 2 + l)
                dve.tensor_tensor(out=mixed_sum if l == 0 else bias_tab[:, 1:N + 1, 2 * G], in0=mixed_sum,
                                  in1=agg[:, l, :], op=ALU.add).then_inc(mixed_step if l == 0 else bias_tab_done, 1)
            dve.wait_ge(mix1_arrived, DMA)
            dve.wait_ge(mix2T_done, 2)
            mix_matrices(first)
            split_y(first)
            steps(dve, lambda t: None if t is first else one(t))
            b = N - 1
            for g in range(G):
                dve.wait_ge(z_relaid, RELAY * (b + 1))
                if g == 0:
                    dve.wait_ge(conv3_done, G * (b - 1))
                split(z_split, 2 * (b + g), z_hi[b % 2][:, g, 1:S + 1], z_lo[b % 2][:, g, 1:S + 1], z_tap[:, g, :])

        @block.tensor
        def _(pe):
            def conv_tile(g, bank, hi, lo, w_hi, w_lo, done):
                n = 0
                for j in range(JB):
                    for w, a in ((w_hi, hi), (w_hi, lo), (w_lo, hi)):
                        last = pe.matmul(ps[:, bank, :], w[:, j, g, :], a[:, g, j:j + S], start=(n == 0),
                                         stop=(n == 3 * JB - 1))
                        n += 1
                last.then_inc(done, 1)

            def conv0_tile(t, g):
                b = t.i
                if t is first:
                    pe.wait_ge(x_split, 2 * (g + 1))
                elif g == 0:
                    pe.wait_ge(x_split, x_splits(b))
                    wait(pe, z_evac, 2 * (b - 1))
                if g == 2:
                    wait(pe, out_evac, G * PH * (b - 3) + 2 * PH)
                if t.at(1) or t.at(2) and g >= 2:
                    pe.wait_ge(y_evac, G * (b - 1) + g + 1)
                conv_tile(g, g, x_hi[t.par(0)], x_lo[t.par(0)], taps0_hi, taps0_lo, conv0_done)

            def mix(t):
                b = t.i - 1
                pe.wait_ge(y_split, 2 * b + 2)
                pe.wait_ge(prod_split, 2 * b + 2)
                for q in range(PH):
                    bank = (4, 5, 0, 1)[q]
                    if q == 0:
                        wait(pe, out_evac, G * PH * (b - 1))
                    if q == 2 and t.has(0):
                        pe.wait_ge(y_evac, G * t.i + 2)
                    for n, (w, a) in enumerate(((prod_hi, y_hi), (prod_hi, y_lo), (prod_lo, y_hi))):
                        last = pe.matmul(ps[:, bank, :], w[:, :], a[:, q, :], start=(n == 0), stop=(n == 2))
                    last.then_inc(mix_done, 1)

            def product(t):
                b = t.i - 1
                pe.wait_ge(mats_step, 2 * K * (b + 1))
                wait(pe, prod_split, 2 * b)
                pe.matmul(ps[:, 6, 0:C], mat1[:, :], mat2T[:, :], start=True, stop=True).then_inc(prod_done, 1)

            def conv3(t):
                b = t.i - 2
                if not t.at(N + 1):
                    pe.wait_ge(z_split, 2 * b + 2)
                for g in range(G):
                    if t.at(N + 1):
                        pe.wait_ge(z_split, 2 * (b + g + 1))
                    if g == 0 and t.has(0):
                        pe.wait_ge(y_evac, G * t.i + 4)
                    if g == 0 and not t.has(0):
                        wait(pe, out_evac, G * PH * b)
                    if g == 2 and t.has(-1):
                        pe.wait_ge(z_evac, 2 * (b + 1) + 1)
                    conv_tile(g, 2 + g, z_hi[t.par(0)], z_lo[t.par(0)], taps3_hi, taps3_lo, conv3_done)

            def one(t):
                for g in range(G):
                    if t.has(0) and t is not first:
                        conv0_tile(t, g)
                        if t.at(1) and g < JB:
                            tap_windows(1, g)
                    if g == 1 and t.has(-1):
                        product(t)
                if t.at(1):
                    pe.wait_ge(taps_lo_done[1], JB)
                if t.has(-1):
                    mix(t)
                if t.has(-2):
                    conv3(t)

            def tap_windows(l, j):
                pe.wait_ge(windows_cut[l], PH * (j + 1))
                if l == 1 and j == 0:
                    pe.wait_ge(mix2T_done, 2)
                if l == 1 and j == 2:
                    pe.wait_ge(bias_tab_done, 3)
                for q in range(PH):
                    last = pe.transpose(ps[:, window_bank(l, j), 128 * q:128 * q + 128], windows[l][:, j, q, :],
                                        ident[:, :])
                last.then_inc(windows_done[l], 1)

            def conv_bias(l):
                pe.wait_ge(ctx_rep_done[l], 2 * PH)
                for g in range(G):
                    o = ps[:, 7, 256 + 128 * l + N * g:256 + 128 * l + N * g + N]
                    pe.matmul(o, ctx_rep[l][:, 128 * g:128 * g + 128], condT, start=True, stop=False)
                    last = pe.matmul(o, side_rep[l][:, 128 * g:128 * g + 128], ones[0:1, 0:N], start=False, stop=True)
                last.then_inc(bias_psum[l], 1)

            def hidden(m):
                if m == 0:
                    pe.wait_ge(mlp_w_arrived, 4 * DMA)
                    pe.wait_ge(mlp_arrived, 10 * DMA)
                else:
                    pe.wait_ge(hidden_done, 2)
                for l in range(2):
                    at = 64 + 32 * (2 * m + l)
                    last = pe.matmul(ps[:, 6, at:at + 32], mlp_w[l][m], condT if m == 0 else hid[l][0],
                                     start=True, stop=True)
                last.then_inc(hidden_psum, 1)

            def logits():
                pe.wait_ge(hidden_done, 4)
                for l in range(2):
                    o = ps[0:N, 6, 192 + K * l:192 + K * l + K]
                    pe.matmul(o, hid[l][1], key_w[l], start=True, stop=False)
                    last = pe.matmul(o, ones[0:1, 0:N], key_b[l], start=False, stop=True)
                last.then_inc(logits_psum, 1)

            pe.wait_ge(ident_step, 3)
            pe.wait_ge(cond_arrived, DMA)
            pe.transpose(ps[:, 6, 0:N], cond_in, ident[0:N, 0:N]).then_inc(condT_psum, 1)
            pe.wait_ge(ctx_w_in[0], DMA)
            pe.transpose(ps[:, 7, 0:128], ctx_in[0], ident[:, :]).then_inc(ctxT_psum[0], 1)
            for j in range(JB):
                tap_windows(0, j)
            pe.wait_ge(condT_done, 1)
            hidden(0)
            pe.wait_ge(taps_lo_done[0], JB)
            conv0_tile(first, 0)
            hidden(1)
            conv_bias(0)
            conv0_tile(first, 1)
            logits()
            pe.wait_ge(ctx_w_in[1], DMA)
            pe.wait_ge(bias_tab_done, 1)
            pe.transpose(ps[:, 7, 128:256], ctx_in[1], ident[:, :]).then_inc(ctxT_psum[1], 1)
            pe.wait_ge(mix2_arrived, DMA)
            for h in range(2):
                for k in range(4):
                    last = pe.transpose(ps[:, 4 + h, 128 * k:128 * k + 128], mix2_in[:, 4 * h + k, :], ident[:, :])
                last.then_inc(mix2T_psum, 1)
            conv0_tile(first, 2)
            conv_bias(1)
            pe.wait_ge(att_step, 4)
            for l in range(2):
                last = pe.transpose(ps[0:K, 6, 256 + N * l:256 + N * l + N], att[l], ident[0:N, 0:N])
            last.then_inc(attT_psum, 1)
            pe.wait_ge(spread_done, 1)
            pe.wait_ge(y_evac, 1)
            pe.matmul(ps[:, 0, :], ones[0:N, :], spread[:, :, :].rearrange("n m k -> n (m k)"), start=True, stop=True)\
              .then_inc(att_tab_psum, 1)
            conv0_tile(first, 3)
            pe.wait_ge(attT_done, 1)
            for l in range(2):
                last = pe.matmul(ps[:, 6, 320 + N * l:320 + N * l + N], bias_k[l], attT_sb[:, l, :], start=True, stop=True)
            last.then_inc(agg_psum, 1)
            pe.wait_ge(agg_done, 1)
            pe.wait_ge(mix2T_done, 2)
            pe.wait_ge(bias_tab_done, 2)
            for k in range(K):
                last = pe.matmul(ps[:, 7, N * k:N * k + N], mix2_wT[:, k, :], agg[:, 0, :], start=True, stop=True)
            last.then_inc(mixed_psum, 1)
            pe.wait_ge(att_tab_done, 1)
            steps(pe, one)


_INS = ['x', 'cond_128', 'fside_S_0', 'L0_cond_weight', 'L0_cond_c_weight',
        'L1_cond_W0', 'L1_cond_b0', 'L1_cond_W1', 'L1_cond_b1', 'L1_cond_W2', 'L1_cond_b2', 'L1_cond_weight',
        'L1_cond_bias_k', 'L2_cond_W0', 'L2_cond_b0', 'L2_cond_W1', 'L2_cond_b1', 'L2_cond_W2', 'L2_cond_b2',
        'L2_cond_weight', 'L2_cond_bias_k', 'L3_cond_weight', 'L3_cond_c_weight']


def kernel(**inputs):
    import numpy as _np
    import concourse.bacc as _bacc
    from concourse import mybir as _mybir
    from concourse.bass_utils import run_bass_kernel_spmd as _run

    nc = _bacc.Bacc("TRN2", target_bir_lowering=False, num_devices=1)
    arrays, a = {}, {}
    for name in _INS:
        v = _np.ascontiguousarray(inputs[name])
        if v.ndim == 4:
            v = v.reshape(v.shape[:3])
        arrays[f"in_{name}"] = v
        a[name] = nc.dram_tensor(f"in_{name}", v.shape, _mybir.dt.from_np(v.dtype), kind="ExternalInput").ap()
    out = nc.dram_tensor("out", (N, C, L), F32, kind="ExternalOutput").ap()
    mixes = [[a[f"L{l}_cond_{n}"] for n in ("W0", "b0", "W1", "b1", "W2", "b2", "weight", "bias_k")] for l in (1, 2)]
    conditioned_residual_kernel(nc, a['x'], a['cond_128'], a['fside_S_0'], a['L0_cond_weight'], a['L0_cond_c_weight'],
                                mixes[0], mixes[1], a['L3_cond_weight'], a['L3_cond_c_weight'], out)
    r = _run(nc, [arrays], core_ids=[0])
    return r.results[0]["out"]
```

```python
from contextlib import ExitStack

import concourse.bass as bass
from concourse import mybir

F32 = mybir.dt.float32
F32R = mybir.dt.float32r
ALU = mybir.AluOpType
ACT = mybir.ActivationFunctionType
AX = mybir.AxisListType

N, C, L = 32, 128, 2048
G = 4
GC = C // G
TAPS, PAD = 9, 4
PH = C // GC
S = L // PH
JB = 3
SLOTS = PH * JB + PH - 1
FIRST = PH - 1
K = 8
D = 128
DMA = 16
RELAY = G * DMA
ATT = 2 * K
BIAS = 2 * G + 1


def conditioned_residual_kernel(nc, x, cond, side, conv0_w, ctx0_w, mix1, mix2, conv3_w, ctx3_w, out):
    ctx = ExitStack()
    with ctx:
        def sb(name, shape, dt=F32):
            return ctx.enter_context(nc.sbuf_tensor(name, shape, dt))

        def sem(name):
            return ctx.enter_context(nc.semaphore(name))

        x_in = [sb(f"x_in{i}", [C, L]) for i in range(2)]
        x_phase = sb("x_phase", [C, PH, S])
        x_tap = sb("x_tap", [C, G, S])
        x_hi = [sb(f"x_hi{i}", [C, G, S + 2], F32R) for i in range(2)]
        x_lo = [sb(f"x_lo{i}", [C, G, S + 2], F32R) for i in range(2)]
        y_tap = sb("y_tap", [C, G, S])
        y_phase = sb("y_phase", [C, PH, S])
        y_hi = sb("y_hi", [C, PH, S], F32R)
        y_lo = sb("y_lo", [C, PH, S], F32R)
        z_phase = sb("z_phase", [C, PH, S])
        z_tap = sb("z_tap", [C, G, S])
        z_hi = [sb(f"z_hi{i}", [C, G, S + 2], F32R) for i in range(2)]
        z_lo = [sb(f"z_lo{i}", [C, G, S + 2], F32R) for i in range(2)]
        out_sb = [sb(f"out_sb{i}", [C, L]) for i in range(2)]

        taps0_hi = sb("taps0_hi", [C, JB, G, C], F32R)
        taps0_lo = sb("taps0_lo", [C, JB, G, C], F32R)
        taps3_hi = sb("taps3_hi", [C, JB, G, C], F32R)
        taps3_lo = sb("taps3_lo", [C, JB, G, C], F32R)
        mix1_w = sb("mix1_w", [C, K, C])
        mix2_wT = sb("mix2_wT", [C, K, C])
        mat1 = sb("mat1", [C, C])
        mat2T = sb("mat2T", [C, C])
        acc1 = sb("acc1", [C, C])
        acc2 = sb("acc2", [C, C])
        prod_hi = sb("prod_hi", [C, C], F32R)
        prod_lo = sb("prod_lo", [C, C], F32R)
        att_tab = sb("att_tab", [C, N, ATT])
        att_cur = [sb(f"att_cur{i}", [C, ATT]) for i in range(2)]
        agg = sb("agg", [C, 2, N])
        bias_tab = sb("bias_tab", [C, N + 2, BIAS])
        bias_cur = [sb(f"bias_cur{i}", [C, BIAS]) for i in range(2)]
        ident = sb("ident", [C, C])
        ones = sb("ones", [GC, C])

        o0, o1 = out_sb[0], out_sb[1]
        padded0 = o0[:, 0:GC * SLOTS].rearrange("o (c k) -> o c k", k=SLOTS)
        conv0_in = o0[:, 480:480 + GC * TAPS].rearrange("o (c k) -> o c k", k=TAPS)
        padded3 = o0[:, 768:768 + GC * SLOTS].rearrange("o (c k) -> o c k", k=SLOTS)
        conv3_in = o0[:, 1248:1248 + GC * TAPS].rearrange("o (c k) -> o c k", k=TAPS)
        windows = [b[:, :, :].rearrange("c p s -> c (p s)")[:, 0:JB * PH * C]
                   .rearrange("o (j q m) -> o j q m", j=JB, q=PH) for b in (z_phase, z_tap)]
        z3 = z_tap[:, 3, :]
        ctx_in = [z3[:, 128 * l:128 * l + 128] for l in range(2)]
        condT = z3[:, 256:256 + N]
        cond_in = z3[0:N, 288:416]
        ctx_rep = [o1[:, 512 * l:512 * l + 512] for l in range(2)]
        side_groups = o0[0:G, 1920:1920 + GC]
        side_steps = o0[0:GC, 1536:1536 + G * N].rearrange("o (g n) -> o g n", g=G)
        repeat = [o0[0:GC, 1664 + C * l:1664 + C * l + C] for l in range(2)]
        mlp_w = [[o1[:, 1024 + 256 * l + 128 * m:1152 + 256 * l + 128 * m] for m in range(2)] for l in range(2)]
        mlp_b = [[o1[:, 1536 + 2 * l + m:1537 + 2 * l + m] for m in range(2)] for l in range(2)]
        key_w = [o1[:, 1544 + K * l:1544 + K * l + K] for l in range(2)]
        key_b = [o1[0:1, 1560 + K * l:1560 + K * l + K] for l in range(2)]
        bias_k = [o1[0:K, 1576 + 128 * l:1704 + 128 * l] for l in range(2)]
        hid = [[o1[:, 1832 + 32 * (2 * l + m):1864 + 32 * (2 * l + m)] for m in range(2)] for l in range(2)]
        mixed_terms = o0[:, 0:N * K].rearrange("c (n k) -> c n k", k=K)
        mixed_sum = o0[:, 480:480 + N]
        soft = sb("soft", [N, 64])
        att_exp = [soft[:, K * l:K * l + K] for l in range(2)]
        att = [soft[:, 16 + K * l:16 + K * l + K] for l in range(2)]
        att_max = [soft[:, 32 + l:33 + l] for l in range(2)]
        att_sum = [soft[:, 34 + l:35 + l] for l in range(2)]
        att_inv = [soft[:, 36 + l:37 + l] for l in range(2)]
        attT_sb = sb("attT_sb", [K, 2, N])
        spread = sb("spread", [N, N, 2 * K])
        mix2_in = y_tap[:, G // 2:G, :].rearrange("o g (k i) -> o (g k) i", i=C)

        ps = ctx.enter_context(nc.psum_tensor("ps", [C, 8, 512], F32))

        conv_w_in = [sem(f"conv_w_in{l}") for l in range(2)]
        ctx_w_in = [sem(f"ctx_w_in{l}") for l in range(2)]
        cond_arrived = sem("cond_arrived")
        side_in = sem("side_in")
        repeat_done = sem("repeat_done")
        sideT_psum = sem("sideT_psum")
        side_steps_done = sem("side_steps_done")
        hidden_w_in = [sem(f"hidden_w_in{m}") for m in range(2)]
        hidden_b_in = sem("hidden_b_in")
        key_w_in = sem("key_w_in")
        key_b_in = sem("key_b_in")
        bias_k_in = sem("bias_k_in")
        mix1_arrived = sem("mix1_arrived")
        mix2_arrived = sem("mix2_arrived")
        ident_step = sem("ident_step")
        padded_step = [sem(f"padded_step{l}") for l in range(2)]
        windows_cut = [sem(f"windows_cut{l}") for l in range(2)]
        windows_done = [sem(f"windows_done{l}") for l in range(2)]
        taps_hi_done = [sem(f"taps_hi_done{l}") for l in range(2)]
        taps_lo_done = [sem(f"taps_lo_done{l}") for l in range(2)]
        condT_psum = sem("condT_psum")
        condT_done = sem("condT_done")
        ctxT_psum = sem("ctxT_psum")
        ctx_rep_done = sem("ctx_rep_done")
        gelu_tables = sem("gelu_tables")
        bias_psum = sem("bias_psum")
        bias_tab_done = sem("bias_tab_done")
        hidden_psum = sem("hidden_psum")
        hidden_done = sem("hidden_done")
        logits_psum = sem("logits_psum")
        max_done = sem("max_done")
        exp_done = sem("exp_done")
        att_step = sem("att_step")
        spread_done = sem("spread_done")
        attT_psum = sem("attT_psum")
        attT_done = sem("attT_done")
        att_tab_psum = sem("att_tab_psum")
        att_tab_done = sem("att_tab_done")
        agg_psum = sem("agg_psum")
        agg_done = sem("agg_done")
        mixed_psum = sem("mixed_psum")
        mixed_step = sem("mixed_step")
        mixed_first = sem("mixed_first")
        mix2T_psum = sem("mix2T_psum")
        mix2T_done = sem("mix2T_done")
        halo_done = sem("halo_done")

        x0_halves = [sem(f"x0_half{h}") for h in range(2)]
        x0_relaid = [sem(f"x0_relaid{g}") for g in range(G)]
        x_loaded = [sem(f"x_loaded{i}") for i in range(2)]
        x_phased = sem("x_phased")
        x_relaid = sem("x_relaid")
        x_split = sem("x_split")
        conv0_done = sem("conv0_done")
        y_evac = sem("y_evac")
        y_relaid = sem("y_relaid")
        y_split = sem("y_split")
        mats_step = sem("mats_step")
        cur_done = sem("cur_done")
        prod_done = sem("prod_done")
        prod_split = sem("prod_split")
        mix_done = sem("mix_done")
        z_evac = sem("z_evac")
        z_relaid = sem("z_relaid")
        z_split = sem("z_split")
        conv3_done = sem("conv3_done")
        bias_done = sem("bias_done")
        out_evac = sem("out_evac")
        out_evac_half = sem("out_evac_half")
        out_stored = [sem(f"out_stored{i}") for i in range(2)]

        block = ctx.enter_context(nc.Block())

        def wait(eng, s, value):
            if not isinstance(value, int) or value > 0:
                eng.wait_ge(s, value)

        class Step:

            def __init__(self, half, parity):
                self.half, self.parity, self.i = half, parity, 2 * half + parity

            def has(self, d):
                return not isinstance(self.half, int) or 0 <= self.i + d < N

            def early(self, d, fill):
                return isinstance(self.half, int) and self.i + d < fill

            def at(self, i):
                return isinstance(self.half, int) and self.i == i

            def par(self, d):
                return (self.parity + d) % 2

            def pair(self, d):
                return self.half + (self.parity + d) // 2

        FILL_X, FILL_Y, FILL_Z = 4, 2, 1
        LOOP = (2, (N - 4) // 2)

        def steps(eng, one):
            for i in range(2 * LOOP[0]):
                one(Step(i // 2, i % 2) if i else first)
            with eng.Fori(LOOP[0], LOOP[1]) as half:
                one(Step(half, 0))
                one(Step(half, 1))
            for i in range(2 * LOOP[1], N + 2):
                one(last_full if i == N - 1 else Step(i // 2, i % 2))

        first = Step(0, 0)
        last_full = Step((N - 1) // 2, (N - 1) % 2)

        REPEAT = ("d (g o q) -> d g q o", "d (g q o) -> d g q o")

        def window_bank(l, j):
            return (j, (4, 5, 7)[j])[l]

        def mix_banks(t):
            return (4, 5, 6, 7) if t.at(1) else (4, 5, 0, 1) if t.has(0) else (6, 7, 0, 1)

        def scalar_phases(t, g):
            return PH if t.has(0) else PH - 1 if t.at(N + 1) and g < G - 1 else PH // 2

        def x_splits(b):
            return 2 * (b + G)

        @block.sync
        def _(sp):
            def count(value):
                return value if isinstance(value, int) else sp.snap(sp.to_reg(value))

            def load_x(t, d):
                b, read = count(t.i + d), count(t.i + d - 1)
                src = x[b]
                wait(sp, x_phased, read)
                sp.dma_start(x_in[t.par(d)][:, :], src).then_inc(x_loaded[t.par(d)], DMA)

            def relay_x(t, d):
                b = t.i + d
                written, read = count(b + 1), 0 if t is first and d == 0 else count(x_splits(b - 1))
                wait(sp, x_split, read)
                wait(sp, x_phased, written)
                for g in range(G):
                    sp.dma_start(x_tap[:, g, :], x_phase[GC * g:GC * g + GC, :, :])\
                      .then_inc(x0_relaid[g] if t is first and d == 0 else x_relaid, DMA)

            def relay_y(t):
                read, written = count(2 * t.i), [count(G * t.i + g + 1) for g in range(G)]
                wait(sp, y_split, read)
                for g in range(G):
                    wait(sp, y_evac, written[g])
                    sp.dma_start(y_phase[GC * g:GC * g + GC, :, :], y_tap[:, g, :]).then_inc(y_relaid, DMA)

            def relay_z(t):
                written, read = count(2 * t.i), count(2 * (t.i - 1))
                wait(sp, z_evac, written)
                wait(sp, z_split, read)
                for g in range(G):
                    sp.dma_start(z_tap[:, g, :], z_phase[GC * g:GC * g + GC, :, :]).then_inc(z_relaid, DMA)

            def store(t):
                b, written = count(t.i - 3), count(G * PH * (t.i - 2))
                dst = out[b]
                wait(sp, out_evac, written)
                if t.at(N + 1):
                    sp.wait_ge(out_evac_half, PH // 2 * G)
                sp.dma_start(dst, out_sb[t.par(-3)][:, :]).then_inc(out_stored[t.par(-3)], DMA)

            def one(t):
                if t.has(1) and t is not first:
                    relay_x(t, 1)
                if t.has(3):
                    load_x(t, 3)
                if t.has(-3) and t.has(0):
                    store(t)
                if t.has(0):
                    relay_y(t)
                if t.has(-1):
                    relay_z(t)
                if not t.has(0):
                    store(t)

            sp.dma_start(conv0_in, conv0_w).then_inc(conv_w_in[0], DMA)
            for h in range(2):
                sp.dma_start(x_in[0][:, h * L // 2:(h + 1) * L // 2], x[0, :, h * L // 2:(h + 1) * L // 2])\
                  .then_inc(x0_halves[h], DMA)
            relay_x(first, 0)
            load_x(first, 1)
            sp.dma_start(mix2_in, mix2[6].rearrange("k o i -> o k i")).then_inc(mix2_arrived, DMA)
            sp.dma_start(mix1_w[:, :, :], mix1[6].rearrange("k o i -> o k i")).then_inc(mix1_arrived, DMA)
            relay_x(first, 1)
            load_x(first, 2)
            steps(sp, one)
            b = N - 1
            for g in range(G):
                sp.wait_ge(out_evac, G * PH * b + PH * (g + 1))
                sp.wait_ge(out_evac_half, PH // 2 * (G + g + 1))
                sp.dma_start(out[b, GC * g:GC * g + GC, :], out_sb[b % 2][GC * g:GC * g + GC, :])\
                  .then_inc(out_stored[b % 2], DMA)
            sp.wait_ge(out_stored[0], DMA * (N // 2))
            sp.wait_ge(out_stored[1], DMA * (N // 2 - 1 + G))

        def pad_taps(eng, l, src, dst):
            eng.memset(dst, 0.0).then_inc(padded_step[l], 1)
            eng.wait_ge(conv_w_in[l], DMA)
            eng.wait_ge(padded_step[l], 1)
            eng.tensor_copy(dst[:, :, FIRST:FIRST + TAPS], src).then_inc(padded_step[l], 1)
            eng.wait_ge(ident_step, 2)
            eng.wait_ge(padded_step[l], 2)
            for g in range(G):
                r = slice(GC * g, GC * g + GC)
                eng.tensor_tensor(out=dst[r, :, FIRST + PAD], in0=dst[r, :, FIRST + PAD],
                                  in1=ident[r, GC * g:GC * g + GC], op=ALU.add).then_inc(padded_step[l], 1)

        def cut_windows(eng, l, src):
            eng.wait_ge(padded_step[l], 2 + G)
            for j in range(JB):
                for q in range(PH):
                    a = PH * (j - 1) - q + PAD + FIRST
                    eng.tensor_copy(windows[l][:, j, q, :].rearrange("o (c p) -> o c p", p=PH), src[:, :, a:a + PH])\
                       .then_inc(windows_cut[l], 1)

        @block.gpsimd
        def _(pool):
            pool.memset(ident[:, :], 0.0).then_inc(ident_step, 1)
            pool.wait_ge(ident_step, 1)
            pool.affine_select(out=ident[:, :], in_=ident[:, :], compare_op=ALU.not_equal, fill=1.0, base=0,
                               pattern=[[-1, C]], channel_multiplier=1).then_inc(ident_step, 1)
            pool.memset(ones[:, :], 1.0).then_inc(ident_step, 1)
            for l, m in enumerate((mix1, mix2)):
                pool.dma_start(mlp_b[l][0], m[1].rearrange("(c a) -> c a", a=1)).then_inc(hidden_b_in, DMA)
                pool.dma_start(mlp_b[l][1], m[3].rearrange("(c a) -> c a", a=1)).then_inc(hidden_b_in, DMA)
            for buf in x_hi + x_lo + z_hi + z_lo:
                pool.memset(buf[:, :, 0:S + 2:S + 1].bitcast(F32), 0.0).then_inc(halo_done, 1)
            pool.memset(bias_tab[:, :, :], 0.0).then_inc(ident_step, 1)
            pool.wait_ge(ident_step, 2)
            for l in range(2):
                unit = ident[0:GC, 0:GC]
                copies = unit.rearrange("r (a o) -> r a o", a=1).to_broadcast([GC, PH, GC]) if l else \
                    unit.rearrange("r (o a) -> r o a", a=1).to_broadcast([GC, GC, PH])
                pool.tensor_copy(repeat[l].rearrange("r (a b) -> r a b", a=(GC, PH)[l]), copies)\
                    .then_inc(repeat_done, 1)
            for l, m in enumerate((mix1, mix2)):
                pool.dma_start(key_b[l], m[5].rearrange("(a k) -> a k", a=1)).then_inc(key_b_in, DMA)
            for l, m in enumerate((mix1, mix2)):
                pool.dma_start(bias_k[l], m[7]).then_inc(bias_k_in, DMA)
            pad_taps(pool, 1, conv3_in, padded3)
            cut_windows(pool, 1, padded3)

        HALOS = 8

        @block.scalar
        def _(act):
            def phase_x(t, d):
                b = t.i + d
                act.wait_ge(x_loaded[t.par(d)], DMA * (t.pair(d) + t.par(d)))
                if t is first and d == 1:
                    for g in range(G):
                        act.wait_ge(x0_relaid[g], DMA)
                else:
                    act.wait_ge(x_relaid, RELAY * (b - 1))
                act.activation(x_phase[:, :, :], x_in[t.par(d)][:, :].rearrange("c (s p) -> c p s", p=PH),
                               ACT.Copy).then_inc(x_phased, 1)

            def high_x(t, d):
                b, p = t.i + d, t.par(d)
                act.wait_ge(x_relaid, RELAY * b)
                wait(act, conv0_done, G * (b - 1))
                act.wait_ge(x_split, x_splits(b - 1))
                act.activation(x_hi[p][:, :, 1:S + 1], x_tap[:, :, :], ACT.Copy).then_inc(x_split, 1)

            def high_y(t, d):
                b = t.i + d
                act.wait_ge(y_relaid, RELAY * (b + 1))
                wait(act, mix_done, PH * b)
                wait(act, y_split, 2 * b)
                act.activation(y_hi[:, :, :], y_phase[:, :, :], ACT.Copy).then_inc(y_split, 1)

            def high_z(t, d):
                b, p = t.i + d, t.par(d)
                act.wait_ge(z_relaid, RELAY * (b + 1))
                wait(act, conv3_done, G * (b - 1))
                wait(act, z_split, 2 * b)
                act.activation(z_hi[p][:, :, 1:S + 1], z_tap[:, :, :], ACT.Copy).then_inc(z_split, 1)

            def copy_bias(t):
                wait(act, y_evac, G * (t.i - 1))
                wait(act, z_evac, 2 * (t.i - 2))
                wait(act, out_evac, G * PH * (t.i - 3))
                n = 2 * G if t.at(1) else BIAS
                act.activation(bias_cur[t.par(0)][:, 0:n], bias_tab[:, t.i, 0:n], ACT.Copy).then_inc(bias_done, 1)

            def evac_y(t, g):
                b = t.i
                if g == 0:
                    act.wait_ge(bias_done, b + 1)
                    wait(act, y_relaid, RELAY * b)
                act.wait_ge(conv0_done, G * b + g + 1)
                act.activation(y_tap[:, g, :], ps[:, g, :], ACT.Identity,
                               bias=bias_cur[t.par(0)][:, g:g + 1]).then_inc(y_evac, 1)

            def evac_z(t):
                b = t.i - 1
                act.wait_ge(bias_done, t.i + 1)
                if t.at(1):
                    act.wait_ge(mixed_first, 1)
                wait(act, z_relaid, RELAY * b)
                for h in range(2):
                    act.wait_ge(mix_done, PH * b + 2 * h + 2)
                    bank = mix_banks(t)[2 * h]
                    act.activation(z_phase[:, 2 * h:2 * h + 2, :], ps[:, bank:bank + 2, :], ACT.Identity,
                                   bias=bias_cur[t.par(0)][:, 2 * G:BIAS]).then_inc(z_evac, 1)

            def evac_out(t, groups=range(G)):
                b = t.i - 2
                act.wait_ge(bias_done, t.i + 1)
                wait(act, out_stored[t.par(0)], DMA * t.pair(-2))
                o = out_sb[t.par(0)][:, :].rearrange("c (s p) -> c p s", p=PH)
                for g in groups:
                    act.wait_ge(conv3_done, G * b + g + 1)
                    mine = scalar_phases(t, g)
                    for q in range(mine):
                        act.activation(o[GC * g:GC * g + GC, q, :], ps[GC * q:GC * q + GC, 2 + g, :], ACT.Identity,
                                       bias=bias_cur[t.par(0)][GC * q:GC * q + GC, G + g:G + g + 1])\
                           .then_inc(out_evac, PH // mine if q < mine - 1 else PH - (mine - 1) * (PH // mine))

            def taps_high(l, j):
                hi, view = ((taps0_hi, "r g (o q) -> r g q o"), (taps3_hi, "r g (q o) -> r g q o"))[l]
                act.wait_ge(windows_done[l], j + 1)
                act.activation(hi[:, j, :, :].rearrange(view, q=PH),
                               ps[:, window_bank(l, j), :].rearrange("r (q g o) -> r g q o", q=PH, g=G), ACT.Copy)\
                   .then_inc(taps_hi_done[l], 1)

            def gelus(m):
                act.wait_ge(hidden_psum, m + 1)
                act.wait_ge(hidden_b_in, 4 * DMA)
                for l in range(2):
                    act.activation(hid[l][m], ps[:, 6, 64 + 32 * (2 * m + l):96 + 32 * (2 * m + l)], ACT.Gelu,
                                   bias=mlp_b[l][m]).then_inc(hidden_done, 1)

            def one(t):
                if t is not first:
                    copy_bias(t)
                    if t.at(2):
                        high_y(t, -1)
                    after = G - 1 if t.at(2) else 1
                    for g in range(G):
                        if t.has(0):
                            evac_y(t, g)
                        if g == 0 and t.at(2):
                            high_z(t, -2)
                        if g == after and t.early(1, FILL_X):
                            high_x(t, 1)
                        if g == after and t.has(2):
                            phase_x(t, 2)
                if t.has(-1):
                    evac_z(t)
                if t.at(N):
                    evac_out(last_full, range(G // 2, G))
                if t.has(-2):
                    evac_out(t, range(G // 2) if t is last_full else range(G))

            def mix2_transposed(h):
                act.wait_ge(mix2T_psum, h + 1)
                act.activation(mix2_wT[:, 4 * h:4 * h + 4, :].rearrange("i k o -> i (k o)"), ps[:, 4 + h, :],
                               ACT.Copy).then_inc(mix2T_done, 1)

            act.dma_start(cond_in, cond).then_inc(cond_arrived, DMA)
            act.wait_ge(ident_step, 3)
            act.activation(att_cur[0][0:1, 0:1], ones[0:1, 0:1], ACT.Gelu).then_inc(gelu_tables, 1)
            act.dma_start(mlp_w[0][0], mix1[0]).then_inc(hidden_w_in[0], DMA)
            act.dma_start(mlp_w[1][0], mix2[0]).then_inc(hidden_w_in[0], DMA)
            act.dma_start(mlp_w[0][1], mix1[2]).then_inc(hidden_w_in[1], DMA)
            act.dma_start(mlp_w[1][1], mix2[2]).then_inc(hidden_w_in[1], DMA)
            act.dma_start(ctx_in[0], ctx0_w).then_inc(ctx_w_in[0], DMA)
            act.dma_start(ctx_in[1], ctx3_w).then_inc(ctx_w_in[1], DMA)
            act.dma_start(side_groups, side.rearrange("(g o) -> g o", g=G)).then_inc(side_in, DMA)
            for l, m in enumerate((mix1, mix2)):
                act.dma_start(key_w[l], m[4]).then_inc(key_w_in, DMA)
            act.dma_start(conv3_in, conv3_w).then_inc(conv_w_in[1], DMA)
            for j in range(JB):
                taps_high(0, j)
            gelus(0)
            act.wait_ge(ctxT_psum, 2)
            for l in range(2):
                rep = ctx_rep[l].rearrange(REPEAT[l], g=G, q=PH)
                for q in range(PH):
                    act.activation(rep[:, :, q, :], ps[:, 7, 128 * l:128 * l + 128].rearrange("d (g o) -> d g o", g=G),
                                   ACT.Copy).then_inc(ctx_rep_done, 1)
            gelus(1)
            act.wait_ge(max_done, 2)
            for l in range(2):
                act.activation(att_exp[l], ps[0:N, 6, 192 + K * l:192 + K * l + K], ACT.Exp,
                               bias=att_max[l], accum_out=att_sum[l]).then_inc(exp_done, 1)
            phase_x(first, 1)
            act.wait_ge(bias_tab_done, 1)
            copy_bias(first)
            evac_y(first, 0)
            mix2_transposed(0)
            high_x(first, 1)
            mix2_transposed(1)
            for g in range(1, G):
                evac_y(first, g)
            phase_x(first, 2)
            for j in range(JB):
                taps_high(1, j)
            high_y(first, 0)
            steps(act, one)

        @block.vector
        def _(dve):
            def split(done, before, hi, lo, src, high=True):
                if high:
                    dve.tensor_copy(hi, src).then_inc(done, 1)
                dve.wait_ge(done, before + 1)
                dve.tensor_tensor(out=lo, in0=src, in1=hi.bitcast(F32), op=ALU.subtract).then_inc(done, 1)

            def split_x(t, d):
                b, p = t.i + d, t.par(d)
                dve.wait_ge(x_relaid, RELAY * b)
                wait(dve, conv0_done, G * (b - 1))
                split(x_split, x_splits(b - 1), x_hi[p][:, :, 1:S + 1], x_lo[p][:, :, 1:S + 1], x_tap[:, :, :],
                      high=not t.early(d, FILL_X))

            def split_x0(g):
                dve.wait_ge(x0_relaid[g], DMA)
                split(x_split, 2 * g, x_hi[0][:, g, 1:S + 1], x_lo[0][:, g, 1:S + 1], x_tap[:, g, :])

            def split_y(t):
                b = t.i
                dve.wait_ge(y_relaid, RELAY * (b + 1))
                wait(dve, mix_done, PH * b)
                split(y_split, 2 * b, y_hi[:, :, :], y_lo[:, :, :], y_phase[:, :, :], high=not t.early(0, FILL_Y))

            def split_z(t):
                b, p = t.i - 2, t.par(-2)
                dve.wait_ge(z_relaid, RELAY * (b + 1))
                wait(dve, conv3_done, G * (b - 1))
                split(z_split, 2 * b, z_hi[p][:, :, 1:S + 1], z_lo[p][:, :, 1:S + 1], z_tap[:, :, :],
                      high=not t.early(-2, FILL_Z))

            def mix_matrices(t):
                b, cur = t.i, att_cur[t.par(0)]
                dve.tensor_copy(cur[:, :], att_tab[:, b, :]).then_inc(cur_done, 1)
                dve.wait_ge(cur_done, b + 1)
                wait(dve, prod_done, b)
                for k in range(K):
                    for l, (w, mat, acc) in enumerate(((mix1_w, mat1, acc1), (mix2_wT, mat2T, acc2))):
                        src, dst = (acc, mat) if k % 2 else (mat, acc)
                        if k:
                            dve.wait_ge(mats_step, 2 * K * b + 2 * (k - 1) + l + 1)
                        dve.scalar_tensor_tensor(out=dst[:, :], in0=w[:, k, :], scalar=cur[:, K * l + k:K * l + k + 1],
                                                 in1=(src if k else ident)[:, :], op0=ALU.mult, op1=ALU.add)\
                           .then_inc(mats_step, 1)

            def split_product(t, d):
                b = t.i + d
                dve.wait_ge(prod_done, b + 1)
                wait(dve, mix_done, PH * b)
                split(prod_split, 2 * b, prod_hi[:, :], prod_lo[:, :], ps[:, 6, 0:C])

            def evac_half(t, g):
                b = t.i - 2
                if g == 0:
                    dve.wait_ge(bias_done, t.i + 1)
                    dve.wait_ge(out_stored[t.par(0)], DMA * t.pair(-2))
                dve.wait_ge(conv3_done, G * b + g + 1)
                o = out_sb[t.par(0)][:, :].rearrange("c (s p) -> c p s", p=PH)
                mine = scalar_phases(t, g)
                for q in range(mine, PH):
                    dve.tensor_scalar(o[GC * g:GC * g + GC, q, :], ps[GC * q:GC * q + GC, 2 + g, :],
                                      bias_cur[t.par(0)][GC * q:GC * q + GC, G + g:G + g + 1], None, ALU.add)\
                       .then_inc(out_evac_half, PH // 2 // (PH - mine))

            def split_last_z(g):
                b = N - 1
                if g == 0:
                    dve.wait_ge(z_relaid, RELAY * (b + 1))
                    dve.wait_ge(conv3_done, G * (b - 1))
                split(z_split, 2 * (b + g), z_hi[b % 2][:, g, 1:S + 1], z_lo[b % 2][:, g, 1:S + 1], z_tap[:, g, :])

            def one(t):
                if t.at(2):
                    split_product(t, -1)
                if t.has(-2) and not t.at(N + 1):
                    split_z(t)
                if t.at(3):
                    split_product(t, -1)
                if t.has(1):
                    split_x(t, 1)
                if t.has(-1) and t.has(0) and not (t.at(1) or t.at(2) or t.at(3)):
                    split_product(t, -1)
                if t.has(0):
                    mix_matrices(t)
                    if t.at(N - 1):
                        split_product(t, 0)
                    split_y(t)
                if t.at(N):
                    evac_half(t, 0)
                    evac_half(t, 1)
                    split_last_z(0)
                    split_last_z(1)
                    for g in range(2, G):
                        evac_half(t, g)
                        split_last_z(g)
                if t.at(N + 1):
                    for g in range(G):
                        evac_half(t, g)

            def taps_low(l, j):
                hi, lo, view = ((taps0_hi, taps0_lo, "r g (o q) -> r g q o"),
                                (taps3_hi, taps3_lo, "r g (q o) -> r g q o"))[l]
                dve.wait_ge(taps_hi_done[l], j + 1)
                dve.tensor_tensor(out=lo[:, j, :, :].rearrange(view, q=PH),
                                  in0=ps[:, window_bank(l, j), :].rearrange("r (q g o) -> r g q o", q=PH, g=G),
                                  in1=hi[:, j, :, :].rearrange(view, q=PH).bitcast(F32), op=ALU.subtract)\
                   .then_inc(taps_lo_done[l], 1)

            def bias_table(l):
                dve.tensor_copy(bias_tab[:, 2 * l:2 * l + N, G * l:G * l + G],
                                ps[:, 7, 256 + 128 * l:384 + 128 * l].rearrange("c (g n) -> c n g", g=G))\
                   .then_inc(bias_tab_done, 1)

            pad_taps(dve, 0, conv0_in, padded0)
            cut_windows(dve, 0, padded0)
            dve.wait_ge(condT_psum, 1)
            dve.tensor_copy(condT, ps[:, 6, 0:N]).then_inc(condT_done, 1)
            for h in range(2):
                dve.wait_ge(x0_halves[h], DMA)
                half = dve.tensor_copy(x_phase[:, :, h * S // 2:(h + 1) * S // 2],
                                       x_in[0][:, h * L // 2:(h + 1) * L // 2].rearrange("c (s p) -> c p s", p=PH))
            half.then_inc(x_phased, 1)
            for j in range(JB):
                taps_low(0, j)
            dve.wait_ge(halo_done, HALOS)
            split_x0(0)
            split_x0(1)
            dve.wait_ge(logits_psum, 1)
            for l in range(2):
                dve.tensor_reduce(out=att_max[l], in_=ps[0:N, 6, 192 + K * l:192 + K * l + K], axis=AX.X, op=ALU.max,
                                  negate=True).then_inc(max_done, 1)
            split_x0(2)
            dve.wait_ge(sideT_psum, 1)
            dve.tensor_copy(side_steps, ps[0:GC, 4, 0:G].rearrange("o (g a) -> o g a", a=1)
                            .to_broadcast([GC, G, N])).then_inc(side_steps_done, 1)
            split_x0(3)
            for l in range(2):
                dve.wait_ge(exp_done, l + 1)
                dve.reciprocal(att_inv[l], att_sum[l]).then_inc(att_step, 1)
                dve.wait_ge(att_step, 2 * l + 1)
                dve.tensor_scalar(att[l], att_exp[l], att_inv[l], None, ALU.mult).then_inc(att_step, 1)
            dve.wait_ge(att_step, 4)
            dve.tensor_tensor(out=spread[:, :, :],
                              in0=soft[:, 16:32].rearrange("n (a k) -> n a k", a=1).to_broadcast([N, N, 2 * K]),
                              in1=ident[0:N, 0:N].rearrange("n (m a) -> n m a", a=1).to_broadcast([N, N, 2 * K]),
                              op=ALU.mult).then_inc(spread_done, 1)
            dve.wait_ge(bias_psum, 1)
            dve.wait_ge(ident_step, 4)
            bias_table(0)
            bias_table(1)
            dve.wait_ge(attT_psum, 1)
            dve.tensor_copy(attT_sb[:, :, :], ps[0:K, 6, 256:320].rearrange("k (l n) -> k l n", l=2))\
               .then_inc(attT_done, 1)
            dve.wait_ge(att_tab_psum, 1)
            dve.tensor_copy(att_tab[:, :, :], ps[:, 5, :].rearrange("c (n k) -> c n k", n=N)).then_inc(att_tab_done, 1)
            split_x(first, 1)
            dve.wait_ge(agg_psum, 1)
            dve.tensor_copy(agg[:, :, :], ps[:, 6, 320:384].rearrange("c (l n) -> c l n", l=2)).then_inc(agg_done, 1)
            dve.wait_ge(mix1_arrived, DMA)
            dve.wait_ge(mix2T_done, 2)
            mix_matrices(first)
            for j in range(JB):
                taps_low(1, j)
            split_y(first)
            split_product(Step(0, 1), -1)
            dve.wait_ge(mixed_psum, 1)
            dve.wait_ge(att_tab_done, 1)
            dve.tensor_tensor(out=mixed_terms, in0=ps[:, 7, 0:N * K].rearrange("c (k n) -> c n k", k=K),
                              in1=att_tab[:, :, K:2 * K], op=ALU.mult).then_inc(mixed_step, 1)
            dve.wait_ge(mixed_step, 1)
            dve.tensor_reduce(out=mixed_sum, in_=mixed_terms, axis=AX.X, op=ALU.add).then_inc(mixed_step, 1)
            dve.wait_ge(agg_done, 1)
            for l in range(2):
                dve.wait_ge(mixed_step, 2 + l)
                dve.tensor_tensor(out=mixed_sum if l == 0 else bias_tab[:, 1:N + 1, 2 * G], in0=mixed_sum,
                                  in1=agg[:, l, :], op=ALU.add).then_inc(mixed_step if l == 0 else bias_tab_done, 1)
            dve.wait_ge(bias_tab_done, 3)
            dve.tensor_copy(bias_cur[1][:, 2 * G:BIAS], bias_tab[:, 1, 2 * G:BIAS]).then_inc(mixed_first, 1)
            steps(dve, lambda t: None if t is first else one(t))

        @block.tensor
        def _(pe):
            def conv_tile(g, bank, hi, lo, w_hi, w_lo, done):
                n = 0
                for j in range(JB):
                    for w, a in ((w_hi, hi), (w_hi, lo), (w_lo, hi)):
                        last = pe.matmul(ps[:, bank, :], w[:, j, g, :], a[:, g, j:j + S], start=(n == 0),
                                         stop=(n == 3 * JB - 1))
                        n += 1
                last.then_inc(done, 1)

            def conv0_tile(t, g):
                b = t.i
                if t is first:
                    pe.wait_ge(x_split, 2 * (g + 1))
                elif g == 0:
                    pe.wait_ge(x_split, x_splits(b))
                    if not t.at(2):
                        wait(pe, z_evac, 2 * (b - 1))
                if g == 2:
                    wait(pe, out_evac, G * PH * (b - 3) + 2 * PH)
                if t.at(1) or t.at(2) and g >= 2:
                    pe.wait_ge(y_evac, G * (b - 1) + g + 1)
                conv_tile(g, g, x_hi[t.par(0)], x_lo[t.par(0)], taps0_hi, taps0_lo, conv0_done)

            def mix(t):
                b = t.i - 1
                pe.wait_ge(y_split, 2 * b + 2)
                pe.wait_ge(prod_split, 2 * b + 2)
                for q in range(PH):
                    bank = mix_banks(t)[q]
                    if q == 0 and t.has(0):
                        wait(pe, out_evac, G * PH * (b - 1))
                    if q == 0 and t.at(2):
                        pe.wait_ge(z_evac, 1)
                    if q == 3 and t.at(1):
                        pe.wait_ge(mixed_step, 1)
                    if q == 2 and not t.has(0):
                        pe.wait_ge(z_evac, 2 * b)
                    if q == 2 and t.has(0) and not t.at(1):
                        pe.wait_ge(y_evac, G * t.i + 2)
                    for n, (w, a) in enumerate(((prod_hi, y_hi), (prod_hi, y_lo), (prod_lo, y_hi))):
                        last = pe.matmul(ps[:, bank, :], w[:, :], a[:, q, :], start=(n == 0), stop=(n == 2))
                    last.then_inc(mix_done, 1)

            def product(t, d):
                b = t.i + d
                pe.wait_ge(mats_step, 2 * K * (b + 1))
                wait(pe, prod_split, 2 * b)
                if t.at(2):
                    pe.wait_ge(z_evac, 2)
                pe.matmul(ps[:, 6, 0:C], mat1[:, :], mat2T[:, :], start=True, stop=True).then_inc(prod_done, 1)

            def conv3(t, groups=range(G)):
                b = t.i - 2
                if not t.at(N + 1):
                    pe.wait_ge(z_split, 2 * b + 2)
                for g in groups:
                    if t.at(N + 1):
                        pe.wait_ge(z_split, 2 * (b + g + 1))
                    if g == 0 and t.has(0):
                        pe.wait_ge(y_evac, G * t.i + 4)
                    if not t.has(0):
                        pe.wait_ge(out_evac, G * PH * (b - 1) + PH * (g + 1))
                        if t.at(N + 1):
                            pe.wait_ge(out_evac_half, 2 * (g + 1))
                    if g == 2 and t.has(0):
                        pe.wait_ge(z_evac, 2 * (b + 1) + 1)
                    conv_tile(g, 2 + g, z_hi[t.par(0)], z_lo[t.par(0)], taps3_hi, taps3_lo, conv3_done)

            def one(t):
                for g in range(G):
                    if t.has(0) and t is not first:
                        conv0_tile(t, g)
                        if t.at(1) and g == 2:
                            mixed_bias()
                    if g == 1 and t.has(-1) and t.has(0):
                        product(t, -1)
                if t.at(1):
                    pe.wait_ge(taps_lo_done[1], JB - 1)
                if t.has(-1) and not t.at(N):
                    mix(t)
                if t.at(2):
                    pe.wait_ge(taps_lo_done[1], JB)
                if t.at(N - 1):
                    product(t, 0)
                    conv3(t, range(G - 1))
                    mix(Step(N // 2, N % 2))
                    conv3(t, range(G - 1, G))
                elif t.has(-2):
                    conv3(t)

            def tap_windows(l, j):
                pe.wait_ge(windows_cut[l], PH * (j + 1))
                if l == 1 and j == 0:
                    pe.wait_ge(mix2T_done, 2)
                if l == 1 and j == 2:
                    pe.wait_ge(bias_tab_done, 2)
                for q in range(PH):
                    last = pe.transpose(ps[:, window_bank(l, j), 128 * q:128 * q + 128], windows[l][:, j, q, :],
                                        ident[:, :])
                last.then_inc(windows_done[l], 1)

            def mix2_transposes(h):
                pe.wait_ge(mix2_arrived, DMA)
                if h == 1:
                    pe.wait_ge(att_tab_done, 1)
                for k in range(4):
                    last = pe.transpose(ps[:, 4 + h, 128 * k:128 * k + 128], mix2_in[:, 4 * h + k, :], ident[:, :])
                last.then_inc(mix2T_psum, 1)

            def mixed_bias():
                pe.wait_ge(agg_done, 1)
                pe.wait_ge(mix2T_done, 2)
                pe.wait_ge(taps_lo_done[1], JB)
                for k in range(K):
                    last = pe.matmul(ps[:, 7, N * k:N * k + N], mix2_wT[:, k, :], agg[:, 0, :], start=True, stop=True)
                last.then_inc(mixed_psum, 1)

            def conv_biases():
                pe.wait_ge(ctx_rep_done, 2 * PH)
                pe.wait_ge(repeat_done, 2)
                pe.wait_ge(side_steps_done, 1)
                for l in range(2):
                    pe.matmul(ps[:, 7, 256 + 128 * l:384 + 128 * l], repeat[l],
                              side_steps.rearrange("o g n -> o (g n)"), start=True, stop=False)
                    for g in range(G):
                        o = ps[:, 7, 256 + 128 * l + N * g:256 + 128 * l + N * g + N]
                        last = pe.matmul(o, ctx_rep[l][:, 128 * g:128 * g + 128], condT, start=False,
                                         stop=(g == G - 1))
                last.then_inc(bias_psum, 1)

            def hidden(m):
                pe.wait_ge(hidden_w_in[m], 2 * DMA)
                if m == 0:
                    pe.wait_ge(condT_done, 1)
                else:
                    pe.wait_ge(hidden_done, 2)
                for l in range(2):
                    at = 64 + 32 * (2 * m + l)
                    last = pe.matmul(ps[:, 6, at:at + 32], mlp_w[l][m], condT if m == 0 else hid[l][0],
                                     start=True, stop=True)
                last.then_inc(hidden_psum, 1)

            def logits():
                pe.wait_ge(hidden_done, 4)
                pe.wait_ge(key_w_in, 2 * DMA)
                pe.wait_ge(key_b_in, 2 * DMA)
                for l in range(2):
                    o = ps[0:N, 6, 192 + K * l:192 + K * l + K]
                    pe.matmul(o, hid[l][1], key_w[l], start=True, stop=False)
                    last = pe.matmul(o, ones[0:1, 0:N], key_b[l], start=False, stop=True)
                last.then_inc(logits_psum, 1)

            pe.wait_ge(ident_step, 3)
            pe.wait_ge(cond_arrived, DMA)
            pe.transpose(ps[:, 6, 0:N], cond_in, ident[0:N, 0:N]).then_inc(condT_psum, 1)
            for j in range(JB):
                tap_windows(0, j)
            pe.wait_ge(side_in, DMA)
            pe.transpose(ps[0:GC, 4, 0:G], side_groups, ident[0:G, 0:G]).then_inc(sideT_psum, 1)
            hidden(0)
            for l in range(2):
                pe.wait_ge(ctx_w_in[l], DMA)
                pe.transpose(ps[:, 7, 128 * l:128 * l + 128], ctx_in[l], ident[:, :]).then_inc(ctxT_psum, 1)
            hidden(1)
            logits()
            pe.wait_ge(taps_lo_done[0], JB)
            conv0_tile(first, 0)
            conv0_tile(first, 1)
            conv_biases()
            pe.wait_ge(att_step, 4)
            for l in range(2):
                last = pe.transpose(ps[0:K, 6, 256 + N * l:256 + N * l + N], att[l], ident[0:N, 0:N])
            last.then_inc(attT_psum, 1)
            pe.wait_ge(spread_done, 1)
            pe.matmul(ps[:, 5, :], ones[0:N, :], spread[:, :, :].rearrange("n m k -> n (m k)"), start=True, stop=True)\
              .then_inc(att_tab_psum, 1)
            mix2_transposes(0)
            conv0_tile(first, 2)
            mix2_transposes(1)
            pe.wait_ge(attT_done, 1)
            pe.wait_ge(bias_k_in, 2 * DMA)
            for l in range(2):
                last = pe.matmul(ps[:, 6, 320 + N * l:320 + N * l + N], bias_k[l], attT_sb[:, l, :], start=True,
                                 stop=True)
            last.then_inc(agg_psum, 1)
            conv0_tile(first, 3)
            for j in range(JB):
                tap_windows(1, j)
            steps(pe, one)


_INS = ['x', 'cond_128', 'fside_S_0', 'L0_cond_weight', 'L0_cond_c_weight',
        'L1_cond_W0', 'L1_cond_b0', 'L1_cond_W1', 'L1_cond_b1', 'L1_cond_W2', 'L1_cond_b2', 'L1_cond_weight',
        'L1_cond_bias_k', 'L2_cond_W0', 'L2_cond_b0', 'L2_cond_W1', 'L2_cond_b1', 'L2_cond_W2', 'L2_cond_b2',
        'L2_cond_weight', 'L2_cond_bias_k', 'L3_cond_weight', 'L3_cond_c_weight']


def kernel(**inputs):
    import numpy as _np
    import concourse.bacc as _bacc
    from concourse import mybir as _mybir
    from concourse.bass_utils import run_bass_kernel_spmd as _run

    nc = _bacc.Bacc("TRN2", target_bir_lowering=False, num_devices=1)
    arrays, a = {}, {}
    for name in _INS:
        v = _np.ascontiguousarray(inputs[name])
        if v.ndim == 4:
            v = v.reshape(v.shape[:3])
        arrays[f"in_{name}"] = v
        a[name] = nc.dram_tensor(f"in_{name}", v.shape, _mybir.dt.from_np(v.dtype), kind="ExternalInput").ap()
    out = nc.dram_tensor("out", (N, C, L), F32, kind="ExternalOutput").ap()
    mixes = [[a[f"L{l}_cond_{n}"] for n in ("W0", "b0", "W1", "b1", "W2", "b2", "weight", "bias_k")] for l in (1, 2)]
    conditioned_residual_kernel(nc, a['x'], a['cond_128'], a['fside_S_0'], a['L0_cond_weight'], a['L0_cond_c_weight'],
                                mixes[0], mixes[1], a['L3_cond_weight'], a['L3_cond_c_weight'], out)
    r = _run(nc, [arrays], core_ids=[0])
    return r.results[0]["out"]
```
